# Optimizing a Trainium2 kernel written in Bass

```python
import numpy as np
import jax
import jax.numpy as jnp

def _softmax(x, axis=-1):
    return jax.nn.softmax(x, axis=axis)

def _gelu(x):
    return jax.nn.gelu(x, approximate=True)

def _silu(x):
    return jax.nn.silu(x)

def _sigmoid(x):
    return jax.nn.sigmoid(x)

def _layernorm(x, axis=-1, eps=1e-05):
    m = jnp.mean(x, axis=axis, keepdims=True)
    v = jnp.var(x, axis=axis, keepdims=True)
    return (x - m) / jnp.sqrt(v + eps)

def _scatter_add(tgt, idx, src, axis=0):
    return tgt.at[idx].add(src)

def _segment_sum(src, seg, n):
    return jax.ops.segment_sum(src, seg, n)
kernel_name = 'mk_macaron_d1_jaxref_r4_7e7b45'

def setup_inputs(seed: int=0):
    np.random.seed(seed)
    _w = jnp.asarray

    def _L0_attn_setup():
        import jax, jax.numpy as jnp
        import numpy as np
        DT = 0.01
        DAMP_MIN = 0.0005
        BATCH, SEQ, D_IN, N_STATE = (16, 512, 256, 128)
        key = jax.random.key(seed)
        k1, k2, k3, k4, k5 = jax.random.split(key, 5)
        u = jax.random.normal(k1, (BATCH, SEQ, D_IN), jnp.float32)
        A_real = jnp.minimum(jax.random.normal(k2, (N_STATE,), jnp.float32) * 0.1 - DAMP_MIN, -DAMP_MIN)
        A_imag = jax.random.normal(k3, (N_STATE,), jnp.float32)
        B = jax.random.normal(k4, (N_STATE, D_IN), jnp.float32) * 0.02
        C = jax.random.normal(k5, (D_IN, N_STATE), jnp.float32) * 0.02
        return {'u': u, 'A_real': A_real, 'A_imag': A_imag, 'B': B, 'C': C}
    _L0_attn_in = _L0_attn_setup()

    def _L0_ffn_setup():
        import jax, jax.numpy as jnp
        import numpy as np
        B, S, D, E, F = (2, 512, 256, 8, 1024)
        key = jax.random.key(seed)
        ks = jax.random.split(key, 4)
        return {'hidden_states': jax.random.normal(ks[0], (B, S, D), dtype=jnp.float32), 'Wr': jax.random.normal(ks[1], (D, E), dtype=jnp.float32) * (1.0 / np.sqrt(D)), 'W1': jax.random.normal(ks[2], (E, D, F), dtype=jnp.float32) * (1.0 / np.sqrt(D)), 'b1': jnp.zeros((E, F), dtype=jnp.float32), 'W2': jax.random.normal(ks[3], (E, F, D), dtype=jnp.float32) * (1.0 / np.sqrt(F)), 'b2': jnp.zeros((E, D), dtype=jnp.float32)}
    _L0_ffn_in = _L0_ffn_setup()
    _d = {'L0_attn_u': _L0_attn_in['u'], 'L0_attn_A_real': _L0_attn_in['A_real'], 'L0_attn_A_imag': _L0_attn_in['A_imag'], 'L0_attn_B': _L0_attn_in['B'], 'L0_attn_C': _L0_attn_in['C'], 'L0_ffn_Wr': _L0_ffn_in['Wr'], 'L0_ffn_W1': _L0_ffn_in['W1'], 'L0_ffn_b1': _L0_ffn_in['b1'], 'L0_ffn_W2': _L0_ffn_in['W2'], 'L0_ffn_b2': _L0_ffn_in['b2']}
    _x0 = _d['L0_attn_u']
    _d['L0_attn_u'] = jax.random.normal(jax.random.fold_in(jax.random.key(seed), 1), (1, 4096, 256), dtype=_x0.dtype)
    del _x0
    return _d

def reference(L0_attn_u, L0_attn_A_real, L0_attn_A_imag, L0_attn_B, L0_attn_C, L0_ffn_Wr, L0_ffn_W1, L0_ffn_b1, L0_ffn_W2, L0_ffn_b2):

    def _L0_attn_ref(u, A_real, A_imag, B, C):
        import jax, jax.numpy as jnp
        import numpy as np
        DT = 0.01
        DAMP_MIN = 0.0005
        BATCH, SEQ, D_IN, N_STATE = (16, 512, 256, 128)
        'Real-input path of StableResonantSSM.\n\n            Bilinear discretization of diagonal complex A:\n              a_disc = (1 + dt/2 * a) / (1 - dt/2 * a)          (elementwise, A diagonal)\n              B_disc = sqrt(dt) * B / (1 - dt/2 * a)            (row-wise scaling)\n            Recurrence: h_t = a_disc * h_{t-1} + B_disc @ u_t;  y_t = Re(C @ h_t).\n            '
        dt = jnp.float32(DT)
        a = (A_real + 1j * A_imag).astype(jnp.complex64)
        denom = 1.0 - dt / 2 * a
        a_disc = (1.0 + dt / 2 * a) / denom
        B_disc = jnp.sqrt(dt) * B.astype(jnp.complex64) / denom[:, None]
        Bu = jnp.einsum('btd,nd->tbn', u, B_disc)

        def step(h, bu_t):
            h = a_disc * h + bu_t
            return (h, h)
        h0 = jnp.zeros((u.shape[0], a.shape[0]), jnp.complex64)
        _, hs = jax.lax.scan(step, h0, Bu)
        y = jnp.einsum('tbn,dn->btd', hs.real, C)
        return y

    def _L0_ffn_ref(hidden_states, Wr, W1, b1, W2, b2):
        import jax, jax.numpy as jnp
        import numpy as np
        B, S, D, E, F = (2, 512, 256, 8, 1024)
        b, s, d = hidden_states.shape
        e = Wr.shape[1]
        x = hidden_states.reshape(b * s, d)
        router_logits = x @ Wr
        router_probs = jax.nn.softmax(router_logits, axis=-1)
        expert_idx = jnp.argmax(router_probs, axis=-1)
        p_max = jnp.max(router_probs, axis=-1, keepdims=True)

        def expert_mlp(w1, bb1, w2, bb2):
            h = jax.nn.gelu(x @ w1 + bb1, approximate=False)
            return h @ w2 + bb2
        outs = jax.vmap(expert_mlp)(W1, b1, W2, b2)
        onehot = jax.nn.one_hot(expert_idx, e, dtype=x.dtype)
        next_states = jnp.einsum('te,etd->td', onehot, outs)
        out = p_max * next_states
        return out.reshape(b, s, d)
    x = L0_attn_u
    x = x + 0.5 * _L0_ffn_ref(_layernorm(x, axis=-1), L0_ffn_Wr, L0_ffn_W1, L0_ffn_b1, L0_ffn_W2, L0_ffn_b2)
    x = x + _L0_attn_ref(_layernorm(x, axis=-1), L0_attn_A_real, L0_attn_A_imag, L0_attn_B, L0_attn_C)
    x = x + 0.5 * _L0_ffn_ref(_layernorm(x, axis=-1), L0_ffn_Wr, L0_ffn_W1, L0_ffn_b1, L0_ffn_W2, L0_ffn_b2)
    return x

_drawn_inputs = setup_inputs


def setup_inputs(seed=0):
    import zlib

    import numpy as np

    out = dict(_drawn_inputs(seed))
    spreads = {'L0_ffn_b1': (0.0, 0.279), 'L0_ffn_b2': (0.0, 0.1)}
    factors = {}
    for name, (base, spread) in spreads.items():
        noise = np.random.default_rng([zlib.crc32(name.encode()), seed]).standard_normal(out[name].shape)
        drawn = base * np.exp(spread * noise) if base else spread * noise
        out[name] = jnp.asarray(drawn.astype(out[name].dtype))
    for name, factor in factors.items():
        out[name] = (out[name] * factor).astype(out[name].dtype)
    return out
```

```python
from contextlib import ExitStack

import concourse.bass as bass
from concourse import mybir

F32 = mybir.dt.float32
F16 = mybir.dt.float16
BF16 = mybir.dt.bfloat16
I32 = mybir.dt.int32
U32 = mybir.dt.uint32
ALU = mybir.AluOpType
ACT = mybir.ActivationFunctionType
AX = mybir.AxisListType.X
ABSMAX = bass.bass_isa.ReduceOp.absmax

P = 128
T = 4096
D = 256
DC = D // P
E = 8
F = 1024
FC = F // P
N = 128
NJ = T // P
CH = 512
CT = CH // P
NC = T // CH
NT = NJ + E
GR = 4
RING = 4
EPS = 1e-5
DT = 0.01
BIG = 8192.0
SX = 2.0 ** 10
TOP = 2.0 ** 14
HB = float(D)
EXPONENT = 0x7F800000
TINY = 1e-30
WE = DC * F


def hold(engine, held, sem, value):
    engine.wait_ge(sem, value)
    if not isinstance(value, int):
        engine.sem_inc(held, 1)


class Chain:

    def __init__(self, engine, sem, held=None):
        self.engine, self.sem, self.held = engine, sem, held
        self.n = 0
        self.turns = 0

    def link(self, instruction):
        instruction.then_inc(self.sem, 1)
        self.n += 1
        hold(self.engine, self.held, self.sem, self.turns + self.n)

    def loop(self, turns, body):
        start = self.n
        body(0)
        per = self.n - start
        with self.engine.Fori(1, turns) as it:
            self.turns, self.n = it * per, start
            body(it)
        self.turns, self.n = 0, start + per * turns


def macaron(nc, A):
    u, out = A["L0_attn_u"][0], A["out"][0]
    x1_dram = nc.dram_tensor("x_after_ffn1", [T, D], F32, kind="Internal").ap()
    x2_dram = nc.dram_tensor("x_after_ssm", [T, D], F32, kind="Internal").ap()
    ctx = ExitStack()
    with ctx:
        def sb(name, shape, dt=F32):
            return ctx.enter_context(nc.sbuf_tensor(name, shape, dt))

        def sem(name):
            return ctx.enter_context(nc.semaphore(name))

        w1s = sb("w1s", [P, E * 2 * WE], F16)
        w2s = sb("w2s", [P, E * 2 * WE], F16)
        iota_r = sb("iota_r", [P, P])
        part = sb("part", [P, 1])
        part_i = sb("part_i", [P, 1], I32)
        iota_i = sb("iota_i", [P, P], I32)
        ident = sb("ident", [P, P])
        before = sb("before", [P, P], BF16)
        ones = sb("ones", [P, P], BF16)
        one = sb("one", [P, 1])
        rev = sb("rev", [P, E])
        tid = sb("tid", [P, NJ])
        mhalf = sb("mhalf", [P, CT])
        wr = sb("wr", [P, DC, E])
        bt = sb("bt", [P, DC, N])
        ct = sb("ct", [P, D])
        b1t = sb("b1t", [P, E * FC])
        ev = sb("ev", [P, 24])
        turn = sb("turn", [P, 2, CH])
        back = sb("back", [P, 2, CH])
        rho = sb("rho", [P, 1])
        state = sb("state", [P, 2])
        wmax2 = sb("wmax2", [P, 2, 2])
        wall2 = sb("wall2", [P, 2, 2])
        b1max = sb("b1max", [P, E])
        b1all = sb("b1all", [P, E])
        wall = sb("wall", [P, 2 * E])
        wpow = sb("wpow", [P, 2 * E])
        wscale = sb("wscale", [P, 2 * E])
        hpow = sb("hpow", [P, E])
        hscale = sb("hscale", [P, E])
        inv1 = sb("inv1", [P, E])
        inv2 = sb("inv2", [P, E])
        logits = sb("logits", [P, NJ, E])
        nmean = sb("nmean", [P, NJ])
        rstd = sb("rstd", [P, NJ])
        halfp = sb("halfp", [P, NJ])
        sortf = sb("sortf", [P, NT, 3])
        sorti = sb("sorti", [P, NT, 2], I32)
        eid = sb("eid", [P, NT], I32)

        ARENA = 15872
        arena = sb("arena", [P, ARENA])

        def view(at, *shape, dt=F32):
            size = 1
            for s in shape:
                size *= s
            words = size // 2 if dt is F16 else size
            assert at + words <= ARENA
            a = arena[:, at:at + words]
            if dt is not F32:
                a = a.bitcast(dt)
            names = "abcd"[:len(shape)]
            if len(shape) == 1:
                return a
            return a.rearrange("p (" + " ".join(names) + ") -> p " + " ".join(names),
                               **{n: s for n, s in zip(names, shape)})

        stage = [view(k * WE, WE) for k in range(4)]
        xc = [view(8192 + k * CT * D, CT, D) for k in range(2)]
        xnc = [view(10240 + k * CT * D, CT, D) for k in range(2)]
        xtc = view(12288, DC, CH)
        sval = view(8192, NJ, 4, NT)
        onerow = [view(13312 + k * GR * P, GR, P) for k in range(2)]
        rt = [view(14336 + 256 * k, E * NJ) for k in range(6)]
        hb = [view(k * 1024, FC, P) for k in range(2)]
        hs = [view(2048 + k * 1024, 2, FC, P, dt=F16) for k in range(2)]
        xg = [view(4096 + k * D, D) for k in range(RING)]
        xng = [view(5120 + k * D, D) for k in range(2)]
        xts = [view(5632 + k * 256, 2, DC, P, dt=F16) for k in range(2)]
        og = [view(6144 + k * D, D) for k in range(2)]
        b2b = view(6656, E * D)
        xs = [view(k * CT * D, CT, D) for k in range(4)]
        uns = [view(4096 + k * CT * D, CT, D) for k in range(2)]
        uts = view(6144, DC, CH)
        xn3 = [view(7168 + k * CT * D, CT, D) for k in range(2)]
        xt3 = view(9216, DC, CH)
        mod = view(10240, 2, CH)
        zz = view(11264, 2, CH)
        aa = view(12288, 2, CH)
        hr = [view(13312 + k * CH, CH) for k in range(2)]

        recf = sb("recf", [P, RING, 3])
        gidx = sb("gidx", [P, RING], I32)
        sidx = sb("sidx", [P, RING], I32)
        stats = sb("stats", [P, 4, CT, 6])
        mv = sb("mv", [P, 4, CT, 2])
        ve = sb("ve", [P, 4, CT])
        nm = sb("nm", [P, 4, CT])
        rs = sb("rs", [P, 4, CT])

        bank = [ctx.enter_context(nc.psum_tensor(f"bank{k}", [P, 512], F32)) for k in range(8)]

        par_in = sem("par_in")
        xload = [sem(f"xload{k}") for k in range(2)]
        wload = [sem(f"wload{k}") for k in range(4)]
        iota_done = sem("iota_done")
        const_done = sem("const_done")
        par_t = sem("par_t")
        par_sb = sem("par_sb")
        dve_chain = sem("dve_chain")
        pool_chain = sem("pool_chain")
        pool_held, act_held, dve_held = sem("pool_held"), sem("act_held"), sem("dve_held")
        rho_in = sem("rho_in")
        rho_out = sem("rho_out")
        a_stats = sem("a_stats")
        a_xn = sem("a_xn")
        a_t = sem("a_t")
        a_xt = sem("a_xt")
        a_lg = sem("a_lg")
        a_lgsb = sem("a_lgsb")
        a_rstd = sem("a_rstd")
        w_max = sem("w_max")
        w_all = sem("w_all")
        w_sc = sem("w_sc")
        w_hi = sem("w_hi")
        w_ws = sem("w_ws")
        w_lo = sem("w_lo")
        b1_max = sem("b1_max")
        b1_all = sem("b1_all")
        inv_done = sem("inv_done")
        S = {}
        for ph in (1, 2):
            S[ph] = {k: sem(f"{k}_{ph}") for k in (
                "diff exps onehot counts pos row rowused sorted_sb b2in rec sidx xn turned "
                "xt_hi xt m1 gelu h_hi hsplit m2 o_chain o").split()}
            S[ph]["gath"] = [sem(f"gath{k}_{ph}") for k in range(RING)]
            S[ph]["scat"] = [sem(f"scat{k}_{ph}") for k in range(RING)]
        sx = [sem(f"s_load{k}") for k in range(4)]
        s_store = [sem(f"s_store{k}") for k in range(4)]
        s_stats, s_un, s_ut, s_uts, s_g, s_in, s_hr, s_y, s_x2, s_st3, s_xn3, s_t3, s_xt3, s_lg, s_lgsb = (
            sem(n) for n in ("s_stats s_un s_ut s_uts s_g s_in s_hr s_y s_x2 s_st3 s_xn3 s_t3 s_xt3 s_lg "
                             "s_lgsb").split())

        W1 = A["L0_ffn_W1"].rearrange("e (c p) f -> e p c f", p=P)
        W2 = A["L0_ffn_W2"].rearrange("e (c p) d -> e p c d", p=P)
        u_chunks = u.rearrange("(n i p) d -> n p i d", p=P, i=CT)
        x1_chunks = x1_dram.rearrange("(n i p) d -> n p i d", p=P, i=CT)
        x2_chunks = x2_dram.rearrange("(n i p) d -> n p i d", p=P, i=CT)
        ENTRY = NC // 2

        def later(it):
            return not (isinstance(it, int) and it == 0)

        def at(q, n):
            return bass.ds(q * n, n)

        def weight_parts(e, which):
            if which == 0:
                a = w1s[:, bass.ds(e * (2 * WE), 2 * WE)].rearrange("p (h w) -> p h w", h=2)
            else:
                a = w2s[:, bass.ds(e * (2 * WE), 2 * WE)].rearrange("p (f h d) -> p h f d", f=FC, h=2)
            return a[:, 0], a[:, 1]

        def staged(b):
            return stage[b] if b % 2 == 0 else stage[b].rearrange("p (f d) -> p f d", f=FC)

        braw = view(14336, D)
        craw = view(14592, DC, N)
        b1raw = view(14848, P)[0:E * FC]
        araw = sb("araw", [P, 2])
        NPAR = 6
        block = ctx.enter_context(nc.Block())

        @block.sync
        def _(sp):
            sp.dma_start(araw[:, 0:1], A["L0_attn_A_real"].unsqueeze(1)).then_inc(par_in, 16)
            sp.dma_start(araw[:, 1:2], A["L0_attn_A_imag"].unsqueeze(1)).then_inc(par_in, 16)
            sp.dma_start(braw, A["L0_attn_B"]).then_inc(par_in, 16)
            sp.dma_start(craw, A["L0_attn_C"].rearrange("(c p) n -> p c n", p=P)).then_inc(par_in, 16)
            sp.dma_start(wr[:], A["L0_ffn_Wr"].rearrange("(c p) e -> p c e", p=P)).then_inc(par_in, 16)
            sp.dma_start(b1raw, A["L0_ffn_b1"].rearrange("e (c p) -> (e c) p", p=P)).then_inc(par_in, 16)

            def entry(it):
                for k in range(2):
                    if later(it):
                        sp.wait_ge(a_xn, 2 * it - 1 + k)
                    sp.dma_start(xc[k], u_chunks[bass.ds(it * 2 + k, 1)].squeeze(0)).then_inc(xload[k], 16)
                    for b in (2 * k, 2 * k + 1):
                        if later(it):
                            sp.wait_ge(w_lo, 4 * it - 3 + b)
                        src = (W1 if b % 2 == 0 else W2)[bass.ds(it * 2 + k, 1)].squeeze(0)
                        dst = stage[b].rearrange("p (c f) -> p c f", c=DC if b % 2 == 0 else FC)
                        sp.dma_start(dst, src).then_inc(wload[b], 16)
            Chain(sp, None).loop(ENTRY, entry)

            def load_b2(ph):
                sp.wait_ge(S[ph]["sorted_sb"], 1)
                if ph == 1:
                    sp.wait_ge(w_lo, 2 * E)
                sp.dma_start(b2b, A["L0_ffn_b2"].rearrange("e d -> (e d)").partition_broadcast(P)) \
                    .then_inc(S[ph]["b2in"], 16)
            load_b2(1)
            for k in range(RING):
                sp.wait_ge(S[1]["scat"][k], 16 * (NT // RING))
            for c in range(NC):
                if c >= 4:
                    sp.wait_ge(s_store[c % 4], 16 * (c // 4))
                    sp.wait_ge(s_xn3, c - 3)
                sp.dma_start(xs[c % 4], x1_chunks[c]).then_inc(sx[c % 4], 16)
                if c >= 3:
                    sp.wait_ge(s_x2, c - 2)
                    sp.dma_start(x2_chunks[c - 3], xs[(c - 3) % 4]).then_inc(s_store[(c - 3) % 4], 16)
            for c in range(NC - 3, NC):
                sp.wait_ge(s_x2, c + 1)
                sp.dma_start(x2_chunks[c], xs[c % 4]).then_inc(s_store[c % 4], 16)
            load_b2(2)
            for k in range(RING):
                sp.wait_ge(S[2]["scat"][k], 16 * (NT // RING))

        @block.gpsimd
        def _(pool):
            chain = Chain(pool, pool_chain, pool_held)
            pool.iota(iota_i[:], [[1, P]], base=0, channel_multiplier=0).then_inc(iota_done, 1)
            pool.iota(part_i[:], [[0, 1]], base=0, channel_multiplier=1).then_inc(iota_done, 1)
            pool.memset(mhalf[:], -0.5).then_inc(iota_done, 1)
            hold(pool, pool_held, iota_done, 3)
            hold(pool, pool_held, rho_in, 1)
            pool.tensor_tensor(ev[:, 13:14], ev[:, 12:13], mhalf[:, 0:1], ALU.pow).then_inc(rho_out, 1)

            def normalise(k, src, dst, stats_ready, n, done):
                hold(pool, pool_held, stats_ready, n)
                chain.link(pool.tensor_tensor(rs[:, k, :], ve[:, k, :], mhalf[:], ALU.pow))
                for i in range(CT):
                    last = pool.tensor_scalar(dst[:, i, :], src[:, i, :], nm[:, k, i:i + 1], rs[:, k, i:i + 1],
                                              ALU.add, ALU.mult)
                last.then_inc(done, 1)

            def entry(it):
                for k in range(2):
                    if later(it):
                        hold(pool, pool_held, a_t, 2 * it - 1 + k)
                        hold(pool, pool_held, a_rstd, 2 * it - 1 + k)
                    normalise(k, xc[k], xnc[k], a_stats, it * 2 + k + 1, a_xn)
                    hold(pool, pool_held, w_max, it * 4 + 2 * k + 2)
                    pool.partition_all_reduce(wall2[:, k, :], wmax2[:, k, :], P, ABSMAX) \
                        .then_inc(w_all, 1)
                    for b in (2 * k, 2 * k + 1):
                        hold(pool, pool_held, w_ws, it * 4 + b + 1)
                        hi, lo = weight_parts(it * 2 + k, b % 2)
                        pool.tensor_tensor(lo, staged(b), hi, ALU.subtract).then_inc(w_lo, 1)
            chain.loop(ENTRY, entry)
            hold(pool, pool_held, b1_max, 1)
            pool.partition_all_reduce(b1all[:], b1max[:], P, ABSMAX).then_inc(b1_all, 1)

            def ffn(ph, src, dst):
                s = S[ph]
                table = src
                hold(pool, pool_held, s["sorted_sb"], 1)
                if ph == 2:
                    for k in range(4):
                        hold(pool, pool_held, s_store[k], 16 * (NC // 4))
                else:
                    hold(pool, pool_held, w_lo, 2 * E)

                def fetch(q, k):
                    if not isinstance(q, int) or q >= RING:
                        hold(pool, pool_held, s["o"], q - RING + 1)
                    pool.tensor_copy(recf[:, k, :], sortf[:, at(q, 1), :].squeeze(1)).then_inc(s["rec"], 1)
                    pool.tensor_copy(gidx[:, k:k + 1], sorti[:, at(q, 1), 0:1].squeeze(1)).then_inc(s["rec"], 1)
                    hold(pool, pool_held, s["rec"], 2 * q + 2)
                    pool.indirect_dma_start(xg[k], None, table, bass.IndirectOffsetOnAxis(ap=gidx[:, k:k + 1].bitcast(U32), axis=0)) \
                        .then_inc(s["gath"][k], 16)

                def norm(q, k):
                    if not isinstance(q, int) or q >= 2:
                        hold(pool, pool_held, s["turned"], q - 1)
                    hold(pool, pool_held, s["gath"][k], (q - k) * (16 // RING) + 16)
                    pool.tensor_scalar(xng[k % 2], xg[k], recf[:, k, 0:1], recf[:, k, 1:2], ALU.add, ALU.mult) \
                        .then_inc(s["xn"], 1)

                def scatter(q, k):
                    if not isinstance(q, int) or q >= RING:
                        hold(pool, pool_held, s["scat"][k], (q - k) * (16 // RING))
                    pool.tensor_copy(sidx[:, k:k + 1], sorti[:, at(q, 1), 1:2].squeeze(1)).then_inc(s["sidx"], 1)
                    hold(pool, pool_held, s["sidx"], q + 1)
                    hold(pool, pool_held, s["o"], q + 1)
                    pool.indirect_dma_start(dst, bass.IndirectOffsetOnAxis(ap=sidx[:, k:k + 1].bitcast(U32), axis=0),
                                            og[k % 2], None, bounds_check=T - 1, oob_is_err=False) \
                        .then_inc(s["scat"][k], 16)

                def step(q, k):
                    if not isinstance(q, int) or q >= 1:
                        norm(q - 1, (k - 1) % RING)
                    if not isinstance(q, int) or q >= RING:
                        scatter(q - RING, k)
                    if not isinstance(q, int) or q < NT:
                        fetch(q, k)

                for q in range(RING):
                    step(q, q % RING)
                with pool.Fori(1, NT // RING) as it:
                    for k in range(RING):
                        step(it * RING + k, k)
                norm(NT - 1, RING - 1)
                for q in range(NT - RING, NT):
                    scatter(q, q % RING)

            ffn(1, u, x1_dram)
            for c in range(NC + 2):
                if c < NC:
                    if c >= 2:
                        hold(pool, pool_held, s_ut, c - 1)
                    normalise(c % 2, xs[c % 4], uns[c % 2], s_stats, c + 1, s_un)
                if c >= 2:
                    d = c - 2
                    if d >= 2:
                        hold(pool, pool_held, s_t3, d - 1)
                    normalise(2 + d % 2, xs[d % 4], xn3[d % 2], s_st3, d + 1, s_xn3)
            ffn(2, x2_dram, out)

        @block.scalar
        def _(act):
            def entry(it):
                for k in range(2):
                    hold(act, act_held, a_t, it * 2 + k + 1)
                    if later(it) or k:
                        hold(act, act_held, a_lg, it * 2 + k)
                    for d in range(DC):
                        last = act.copy(xtc[:, d, :], bank[2 * k + d][:])
                    last.then_inc(a_xt, 1)
                    for b in (2 * k, 2 * k + 1):
                        hold(act, act_held, w_sc, it * 2 + k + 1)
                        hi, lo = weight_parts(it * 2 + k, b % 2)
                        scale = wscale[:, bass.ds(it * 4 + b, 1)]
                        act.activation(hi, staged(b), ACT.Copy, scale=scale).then_inc(w_hi, 1)
                        hold(act, act_held, w_hi, it * 4 + b + 1)
                        act.activation(stage[b], stage[b], ACT.Copy, scale=scale).then_inc(w_ws, 1)
            Chain(act, None).loop(ENTRY, entry)

            def ffn(ph):
                s = S[ph]
                act.wait_ge(s["diff"], 1)
                act.activation(rt[1], rt[0], ACT.Exp).then_inc(s["exps"], 1)
                act.wait_ge(s["sorted_sb"], 1)
                act.wait_ge(inv_done, 1)

                def step(q, k):
                    e = act.value_load(eid[0:1, at(q, 1)], min_val=0, max_val=E - 1)
                    for half in range(2):
                        act.wait_ge(s["m1"], q * 2 + half + 1)
                        if half == 0 and (not isinstance(q, int) or q >= 2):
                            act.wait_ge(s["hsplit"], q * 2 - 2)
                        for f in range(half * 4, half * 4 + 4):
                            src = bank[2 * (k % 2) + half][:, (f % 4) * P:(f % 4 + 1) * P]
                            last = act.activation(hb[k % 2][:, f, :], src, ACT.Gelu,
                                                  bias=b1t[:, bass.ds(e * FC + f, 1)], scale=inv1[:, bass.ds(e, 1)])
                        last.then_inc(s["gelu"], 1)

                for q in range(RING):
                    step(q, q % RING)
                with act.Fori(1, NT // RING) as it:
                    for k in range(RING):
                        step(it * RING + k, k)
            ffn(1)
            for c in range(NC + 2):
                if c < NC:
                    act.wait_ge(s_ut, c + 1)
                    if c >= 1:
                        act.wait_ge(s_g, c)
                    for d in range(DC):
                        last = act.copy(uts[:, d, :], bank[d][:])
                    last.then_inc(s_uts, 1)
                if c >= 2:
                    d3 = c - 2
                    act.wait_ge(s_t3, d3 + 1)
                    if d3 >= 1:
                        act.wait_ge(s_lg, d3)
                    for d in range(DC):
                        last = act.copy(xt3[:, d, :], bank[2 + d][:])
                    last.then_inc(s_xt3, 1)
            ffn(2)

        @block.vector
        def _(dve):
            chain = Chain(dve, dve_chain, dve_held)
            link = chain.link
            dve.wait_ge(iota_done, 2)
            dve.tensor_copy(iota_r[:], iota_i[:])
            link(dve.tensor_copy(part[:], part_i[:]))
            dve.tensor_scalar(ident[:], iota_r[:], part[:], None, ALU.is_equal).then_inc(const_done, 1)
            dve.tensor_scalar(before[:], iota_r[:], part[:], None, ALU.is_gt)
            dve.memset(ones[:], 1.0)
            dve.memset(one[:], 1.0)
            dve.tensor_scalar(rev[:], iota_r[:, 0:E], -1.0, float(E), ALU.mult, ALU.add)
            link(dve.tensor_scalar(tid[:], iota_r[:, 0:NJ], float(P), -BIG, ALU.mult, ALU.add))
            dve.tensor_scalar(tid[:], tid[:], part[:], None, ALU.add)

            col = lambda k: ev[:, k:k + 1]
            dve.wait_ge(par_in, 16 * NPAR)
            link(dve.tensor_scalar(ev[:, 0:2], araw[:], DT / 2, None, ALU.mult))
            dve.tensor_scalar(col(2), col(0), -1.0, 1.0, ALU.mult, ALU.add)
            dve.tensor_scalar(col(3), col(0), 1.0, None, ALU.add)
            link(dve.tensor_tensor(col(4), col(1), col(1), ALU.mult))
            dve.scalar_tensor_tensor(col(5), col(2), col(2), col(4), ALU.mult, ALU.add)
            link(dve.scalar_tensor_tensor(col(6), col(3), col(2), col(4), ALU.mult, ALU.subtract))
            dve.reciprocal(col(7), col(5))
            link(dve.tensor_tensor(col(8), col(2), col(3), ALU.add))
            link(dve.tensor_tensor(col(9), col(8), col(1), ALU.mult))
            dve.tensor_tensor(col(10), col(6), col(7), ALU.mult)
            link(dve.tensor_tensor(col(11), col(9), col(7), ALU.mult))
            dve.tensor_scalar(col(14), col(2), col(7), DT ** 0.5, ALU.mult, ALU.mult)
            dve.tensor_scalar(col(15), col(1), col(7), DT ** 0.5, ALU.mult, ALU.mult)
            link(dve.tensor_tensor(col(16), col(10), col(10), ALU.mult))
            dve.scalar_tensor_tensor(col(12), col(11), col(11), col(16), ALU.mult, ALU.add).then_inc(rho_in, 1)
            dve.wait_ge(rho_in, 1)
            dve.wait_ge(rho_out, 1)
            dve.tensor_tensor(rho[:], col(12), col(13), ALU.mult)
            dve.tensor_scalar(turn[:, 0, 0:1], col(10), col(13), None, ALU.mult)
            link(dve.tensor_scalar(turn[:, 1, 0:1], col(11), col(13), None, ALU.mult))
            n = 1
            while n < CH:
                c0, s0 = turn[:, 0, 0:n], turn[:, 1, 0:n]
                cn, sn = turn[:, 0, n - 1:n], turn[:, 1, n - 1:n]
                dve.tensor_scalar(back[:, 0, 0:n], s0, sn, None, ALU.mult)
                link(dve.tensor_scalar(back[:, 1, 0:n], c0, sn, None, ALU.mult))
                dve.scalar_tensor_tensor(turn[:, 0, n:2 * n], c0, cn, back[:, 0, 0:n], ALU.mult, ALU.subtract)
                link(dve.scalar_tensor_tensor(turn[:, 1, n:2 * n], s0, cn, back[:, 1, 0:n], ALU.mult, ALU.add))
                n *= 2
            tmp = aa
            dve.tensor_scalar(tmp[:, 0, :], turn[:, 1, :], col(15), None, ALU.mult)
            link(dve.tensor_scalar(tmp[:, 1, :], turn[:, 0, :], col(15), None, ALU.mult))
            dve.scalar_tensor_tensor(back[:, 0, :], turn[:, 0, :], col(14), tmp[:, 0, :], ALU.mult, ALU.subtract)
            dve.scalar_tensor_tensor(back[:, 1, :], turn[:, 1, :], col(14), tmp[:, 1, :], ALU.mult, ALU.add)
            link(dve.memset(state[:], 0.0))
            dve.wait_ge(par_t, 1)
            dve.tensor_copy(bt[:], bank[4][:, 0:DC * N].rearrange("p (c n) -> p c n", c=DC))
            dve.tensor_copy(ct[:], bank[4][:, DC * N:DC * N + D]).then_inc(par_sb, 1)
            link(dve.tensor_copy(b1t[:], bank[5][:, 0:E * FC]))
            dve.tensor_reduce(b1max[:], b1t[:].rearrange("p (e c) -> p e c", c=FC), AX, ALU.max,
                              apply_absolute_value=True).then_inc(b1_max, 1)

            def row_stats(src, k, done):
                for i in range(CT):
                    last = dve.bn_stats(stats[:, k, i, :], src[:, i, :])
                link(last)
                for i in range(CT):
                    last = dve.bn_aggr(mv[:, k, i, :], stats[:, k, i, :])
                link(last)
                dve.tensor_scalar(nm[:, k, :], mv[:, k, :, 0], -1.0, None, ALU.mult)
                dve.tensor_scalar(ve[:, k, :], mv[:, k, :, 1], EPS, None, ALU.add).then_inc(done, 1)

            def entry(it):
                for k in range(2):
                    dve.wait_ge(xload[k], it * 16 + 16)
                    if later(it):
                        dve.wait_ge(a_xn, 2 * it - 1 + k)
                    row_stats(xc[k], k, a_stats)
                    for b in (2 * k, 2 * k + 1):
                        dve.wait_ge(wload[b], it * 16 + 16)
                        dve.tensor_reduce(wmax2[:, k, b % 2:b % 2 + 1], stage[b], AX, ALU.max,
                                          apply_absolute_value=True).then_inc(w_max, 1)
                    dve.wait_ge(a_xn, it * 2 + k + 1)
                    dve.tensor_copy(nmean[:, at(it * 2 + k, CT)], nm[:, k, :])
                    dve.tensor_copy(rstd[:, at(it * 2 + k, CT)], rs[:, k, :]).then_inc(a_rstd, 1)
                    two = at(it * 2 + k, 2)
                    dve.wait_ge(w_all, it * 2 + k + 1)
                    link(dve.tensor_scalar(wall[:, two], wall2[:, k, :], TINY, None, ALU.max))
                    link(dve.tensor_scalar(wpow[:, two].bitcast(I32), wall[:, two].bitcast(I32), EXPONENT, None,
                                           ALU.bitwise_and))
                    link(dve.reciprocal(wscale[:, two], wpow[:, two]))
                    dve.tensor_scalar(wscale[:, two], wscale[:, two], TOP, None, ALU.mult).then_inc(w_sc, 1)
                    dve.wait_ge(a_lg, it * 2 + k + 1)
                    dve.tensor_copy(logits[:, at(it * 2 + k, CT), :],
                                    bank[6][:, k * CT * E:(k + 1) * CT * E].rearrange("p (i e) -> p i e", e=E)) \
                        .then_inc(a_lgsb, 1)
            chain.loop(ENTRY, entry)

            dve.wait_ge(b1_all, 1)
            w2x = lambda t, k: t[:, 0:2 * E].rearrange("p (e k) -> p k e", k=2)[:, k, :]
            link(dve.scalar_tensor_tensor(hpow[:], w2x(wall, 0), HB, b1all[:], ALU.mult, ALU.add))
            link(dve.tensor_scalar(hpow[:].bitcast(I32), hpow[:].bitcast(I32), EXPONENT, None, ALU.bitwise_and))
            link(dve.reciprocal(hscale[:], hpow[:]))
            dve.tensor_scalar(hscale[:], hscale[:], TOP, None, ALU.mult)
            dve.tensor_scalar(inv1[:], w2x(wpow, 0), 1.0 / (TOP * SX), None, ALU.mult)
            link(dve.tensor_scalar(hpow[:], hpow[:], 1.0 / TOP, None, ALU.mult))
            dve.scalar_tensor_tensor(inv2[:], w2x(wpow, 1), 1.0 / TOP, hpow[:], ALU.mult, ALU.mult) \
                .then_inc(inv_done, 1)

            def route(ph):
                s = S[ph]
                je = lambda a: a.rearrange("p (j e) -> p j e", e=E)
                ej = lambda a: a.rearrange("p (e j) -> p e j", e=E)
                swap = lambda a: a.rearrange("p (e j) -> p j e", e=E)
                over_e = lambda a: a.unsqueeze(2).to_broadcast([P, NJ, E])
                top = rt[5][:, 0:NJ]
                first = rt[5][:, NJ:2 * NJ]
                pos = rt[5][:, 2 * NJ:3 * NJ]
                tile = rt[5][:, 3 * NJ:4 * NJ]
                slot = rt[5][:, 4 * NJ:5 * NJ]
                small = lambda k: rt[5][:, 5 * NJ + 8 * k:5 * NJ + 8 * k + 8]
                link(dve.tensor_reduce(top, logits[:], AX, ALU.max))
                dve.tensor_tensor(je(rt[0]), logits[:], over_e(top), ALU.subtract).then_inc(s["diff"], 1)
                link(dve.tensor_tensor(je(rt[2]), logits[:], over_e(top), ALU.is_equal))
                link(dve.tensor_tensor(je(rt[2]), je(rt[2]), rev[:].unsqueeze(1).to_broadcast([P, NJ, E]), ALU.mult))
                link(dve.tensor_reduce(first, je(rt[2]), AX, ALU.max))
                onehot = rt[3][:, 0:E * NJ // 2].bitcast(BF16)
                dve.tensor_tensor(swap(onehot), rev[:].unsqueeze(1).to_broadcast([P, NJ, E]), over_e(first),
                                  ALU.is_equal).then_inc(s["onehot"], 1)
                dve.wait_ge(s["exps"], 1)
                link(dve.tensor_reduce(halfp[:], je(rt[1]), AX, ALU.add))
                link(dve.reciprocal(halfp[:], halfp[:]))
                dve.tensor_scalar(halfp[:], halfp[:], 0.5, None, ALU.mult)
                dve.wait_ge(s["counts"], 1)
                link(dve.tensor_copy(rt[2], bank[5][:, 256:512]))
                link(dve.tensor_tensor_scan(rt[4], one[:].to_broadcast([P, E * NJ]), rt[2], 0.0, ALU.mult, ALU.add))
                dve.tensor_tensor(rt[2], rt[4], rt[2], ALU.subtract)
                ends = ej(rt[4])[:, :, NJ - 1]
                cnt, tiles, tend, shift = small(0), small(1), small(2), small(3)
                dve.tensor_tensor(cnt[:, 1:E], ends[:, 1:E], ends[:, 0:E - 1], ALU.subtract)
                link(dve.tensor_copy(cnt[:, 0:1], ends[:, 0:1]))
                link(dve.tensor_scalar(tiles.bitcast(I32), cnt, float(P - 1), None, ALU.add))
                link(dve.tensor_scalar(tend.bitcast(I32), tiles.bitcast(I32), 7, None, ALU.arith_shift_right))
                link(dve.tensor_copy(tiles, tend.bitcast(I32)))
                link(dve.tensor_tensor_scan(tend, one[:].to_broadcast([P, E]), tiles, 0.0, ALU.mult, ALU.add))
                link(dve.tensor_tensor(tiles, tend, tiles, ALU.subtract))
                link(dve.tensor_tensor(cnt, ends, cnt, ALU.subtract))
                link(dve.scalar_tensor_tensor(shift, tiles, float(P), cnt, ALU.mult, ALU.subtract))
                link(dve.tensor_tensor(rt[2], rt[2], bank[5][:, 0:256], ALU.add))
                link(dve.tensor_tensor(ej(rt[2]), ej(rt[2]), shift.unsqueeze(2).to_broadcast([P, E, NJ]), ALU.add))
                link(dve.tensor_tensor(rt[2], rt[2], onehot, ALU.mult))
                link(dve.tensor_reduce(pos, swap(rt[2]), AX, ALU.add))
                posi = tile.bitcast(I32)
                link(dve.tensor_copy(posi, pos))
                sloti = pos.bitcast(I32)
                link(dve.tensor_scalar(sloti, posi, P - 1, None, ALU.bitwise_and))
                tli = first.bitcast(I32)
                link(dve.tensor_scalar(tli, posi, 7, None, ALU.arith_shift_right))
                dve.tensor_copy(slot, sloti)
                link(dve.tensor_copy(tile, tli))
                ntc = sval[:, 0:2, :, :].rearrange("p a b c -> p (a b c)")[:, 0:NT * E].rearrange("p (q e) -> p q e", e=E)
                link(dve.tensor_tensor(ntc, iota_r[:, 0:NT].unsqueeze(2).to_broadcast([P, NT, E]),
                                       tend.unsqueeze(1).to_broadcast([P, NT, E]), ALU.is_ge))
                eidf = rt[5][:, 5 * NJ + 32:5 * NJ + 32 + NT]
                link(dve.tensor_reduce(eidf, ntc, AX, ALU.add))
                dve.tensor_scalar(eid[:], eidf, float(E - 1), None, ALU.min)
                q1 = sval[:, :, 3, :]
                link(dve.tensor_tensor(q1, iota_r[:, 0:NT].unsqueeze(1).to_broadcast([P, NJ, NT]),
                                       tile.unsqueeze(2).to_broadcast([P, NJ, NT]), ALU.is_equal))
                for k, v in enumerate((tid, nmean, rstd, halfp)):
                    last = dve.tensor_tensor(sval[:, :, k, :], q1, v[:].unsqueeze(2).to_broadcast([P, NJ, NT]), ALU.mult)
                last.then_inc(s["pos"], 1)
                for g in range(NJ // GR):
                    if g >= 2:
                        dve.wait_ge(s["rowused"], g - 1)
                    dve.tensor_tensor(onerow[g % 2], iota_r[:].unsqueeze(1).to_broadcast([P, GR, P]),
                                      slot[:, GR * g:GR * g + GR].unsqueeze(2).to_broadcast([P, GR, P]),
                                      ALU.is_equal).then_inc(s["row"], 1)
                dve.wait_ge(s["rowused"], NJ // GR)
                sp4 = bank[4][:, 0:4 * NT].rearrange("p (k q) -> p k q", k=4)
                dve.tensor_scalar(sorti[:, :, 0], sp4[:, 0, :], BIG, float(T - 1), ALU.add, ALU.min)
                dve.tensor_scalar(sorti[:, :, 1], sp4[:, 0, :], BIG, None, ALU.add)
                dve.tensor_copy(sortf[:].rearrange("p q k -> p k q"), sp4[:, 1:4, :]).then_inc(s["sorted_sb"], 1)

            def ffn(ph):
                s = S[ph]
                dve.wait_ge(s["sorted_sb"], 1)
                dve.wait_ge(s["b2in"], 16)

                def split_x(q, k):
                    dve.wait_ge(s["turned"], q + 1)
                    if not isinstance(q, int) or q >= 2:
                        dve.wait_ge(s["m1"], q * 2 - 2)
                    src = bank[6 + k % 2][:, 0:DC * P].rearrange("p (c t) -> p c t", c=DC)
                    dve.tensor_scalar(xts[k % 2][:, 0], src, SX, None, ALU.mult).then_inc(s["xt_hi"], 1)
                    dve.wait_ge(s["xt_hi"], q + 1)
                    dve.scalar_tensor_tensor(xts[k % 2][:, 1], src, SX, xts[k % 2][:, 0], ALU.mult, ALU.subtract) \
                        .then_inc(s["xt"], 1)

                def split_h(q, k, e):
                    if not isinstance(q, int) or q >= 2:
                        dve.wait_ge(s["m2"], q - 1)
                    for half in range(2):
                        f = slice(4 * half, 4 * half + 4)
                        dve.wait_ge(s["gelu"], q * 2 + half + 1)
                        sc = hscale[:, bass.ds(e, 1)]
                        dve.tensor_scalar(hs[k % 2][:, 0, f, :], hb[k % 2][:, f, :], sc, None, ALU.mult) \
                            .then_inc(s["h_hi"], 1)
                        dve.wait_ge(s["h_hi"], q * 2 + half + 1)
                        dve.scalar_tensor_tensor(hs[k % 2][:, 1, f, :], hb[k % 2][:, f, :], sc,
                                                 hs[k % 2][:, 0, f, :], ALU.mult, ALU.subtract).then_inc(s["hsplit"], 1)

                def result(q, k, e):
                    dve.wait_ge(s["m2"], q + 1)
                    if not isinstance(q, int):
                        dve.wait_ge(s["scat"][(k - 2) % RING], ((q - 2) - (k - 2) % RING) * (16 // RING) + 16)
                    elif q >= 2:
                        dve.wait_ge(s["scat"][(q - 2) % RING], (q - 2) // RING * 16 + 16)
                    o, acc = og[k % 2], bank[4 + k % 2]
                    i2 = inv2[:, bass.ds(e, 1)]
                    dve.scalar_tensor_tensor(o, acc[:, D:2 * D], i2, b2b[:, bass.ds(e * D, D)], ALU.mult, ALU.add) \
                        .then_inc(s["o_chain"], 1)
                    dve.wait_ge(s["o_chain"], q * 2 + 1)
                    dve.scalar_tensor_tensor(o, acc[:, 0:D], i2, o, ALU.mult, ALU.add).then_inc(s["o_chain"], 1)
                    dve.wait_ge(s["o_chain"], q * 2 + 2)
                    dve.scalar_tensor_tensor(o, o, recf[:, k, 2:3], xg[k], ALU.mult, ALU.add).then_inc(s["o"], 1)

                def expert(q):
                    return dve.value_load(eid[0:1, at(q, 1)], min_val=0, max_val=E - 1)

                def step(q, k):
                    if not isinstance(q, int) or q + 2 < NT:
                        split_x(q + 2, (k + 2) % RING)
                    if not isinstance(q, int) or q + 1 < NT:
                        split_h(q + 1, (k + 1) % RING, expert(q + 1))
                    result(q, k, expert(q))

                split_x(0, 0)
                split_x(1, 1)
                split_h(0, 0, expert(0))
                for q in range(RING):
                    step(q, q % RING)
                with dve.Fori(1, NT // RING - 1) as it:
                    for k in range(RING):
                        step(it * RING + k, k)
                for q in range(NT - RING, NT):
                    step(q, q % RING)

            route(1)
            ffn(1)

            for c in range(NC + 3):
                if c < NC:
                    dve.wait_ge(sx[c % 4], 16 * (c // 4) + 16)
                    if c >= 2:
                        dve.wait_ge(s_un, c - 1)
                    row_stats(xs[c % 4], c % 2, s_stats)
                if 1 <= c <= NC:
                    b = c - 1
                    g = bank[4]
                    dve.wait_ge(s_g, b + 1)
                    dve.tensor_tensor(mod[:, 0, :], g[:], turn[:, 0, :], ALU.mult)
                    dve.scalar_tensor_tensor(mod[:, 1, :], g[:], -1.0, turn[:, 1, :], ALU.mult, ALU.mult) \
                        .then_inc(s_in, 1)
                    dve.wait_ge(s_in, b + 1)
                    dve.tensor_tensor_scan(zz[:, 0, :], rho[:].to_broadcast([P, CH]), mod[:, 0, :], state[:, 0:1],
                                           ALU.mult, ALU.add)
                    link(dve.tensor_tensor_scan(zz[:, 1, :], rho[:].to_broadcast([P, CH]), mod[:, 1, :],
                                                state[:, 1:2], ALU.mult, ALU.add))
                    zr, zi = zz[:, 0, CH - 1:CH], zz[:, 1, CH - 1:CH]
                    cl, sl = turn[:, 0, CH - 1:CH], turn[:, 1, CH - 1:CH]
                    dve.tensor_tensor(ev[:, 20:21], zi, sl, ALU.mult)
                    dve.tensor_tensor(ev[:, 21:22], zr, sl, ALU.mult)
                    dve.tensor_tensor(aa[:, 0, :], zz[:, 0, :], back[:, 0, :], ALU.mult)
                    link(dve.tensor_tensor(aa[:, 1, :], zz[:, 1, :], back[:, 1, :], ALU.mult))
                    dve.scalar_tensor_tensor(state[:, 0:1], zr, cl, ev[:, 20:21], ALU.mult, ALU.subtract)
                    dve.scalar_tensor_tensor(state[:, 1:2], zi, cl, ev[:, 21:22], ALU.mult, ALU.add)
                    if b >= 2:
                        dve.wait_ge(s_y, b - 1)
                    dve.tensor_tensor(hr[b % 2], aa[:, 0, :], aa[:, 1, :], ALU.subtract).then_inc(s_hr, 1)
                    dve.wait_ge(s_hr, b + 1)
                if 2 <= c <= NC + 1:
                    b = c - 2
                    dve.wait_ge(s_y, b + 1)
                    for h in range(2):
                        rows = xs[b % 4][:, 2 * h:2 * h + 2, :]
                        last = dve.tensor_tensor(rows, rows, bank[6 + h][:].rearrange("p (i d) -> p i d", d=D), ALU.add)
                    last.then_inc(s_x2, 1)
                    dve.wait_ge(s_x2, b + 1)
                    if b >= 2:
                        dve.wait_ge(s_xn3, b - 1)
                    row_stats(xs[b % 4], 2 + b % 2, s_st3)
                if c >= 3:
                    b = c - 3
                    dve.wait_ge(s_xn3, b + 1)
                    dve.tensor_copy(nmean[:, b * CT:(b + 1) * CT], nm[:, 2 + b % 2, :])
                    dve.tensor_copy(rstd[:, b * CT:(b + 1) * CT], rs[:, 2 + b % 2, :])
                    dve.wait_ge(s_lg, b + 1)
                    dve.tensor_copy(logits[:, b * CT:(b + 1) * CT, :],
                                    bank[5][:, 0:CT * E].rearrange("p (i e) -> p i e", e=E)).then_inc(s_lgsb, 1)
            dve.wait_ge(s_lgsb, NC)
            route(2)
            ffn(2)

        @block.tensor
        def _(pe):
            pe.wait_ge(const_done, 1)
            pe.wait_ge(par_in, 16 * NPAR)
            for c in range(DC):
                pe.transpose(bank[4][:, c * N:(c + 1) * N], braw[:, c * P:(c + 1) * P], ident[:])
                pe.transpose(bank[4][:, DC * N + c * P:DC * N + (c + 1) * P], craw[:, c, :], ident[:])
            pe.transpose(bank[5][:, 0:E * FC], b1raw, ident[0:E * FC, 0:E * FC]).then_inc(par_t, 1)

            def turn_rows(src, banks, done):
                for d in range(DC):
                    for i in range(CT):
                        last = pe.transpose(banks[d][:, i * P:(i + 1) * P], src[:, i, d * P:(d + 1) * P], ident[:])
                last.then_inc(done, 1)

            def route_logits(src, dst, done):
                for i in range(CT):
                    for d in range(DC):
                        last = pe.matmul(dst[:, i * E:(i + 1) * E], src[:, d, i * P:(i + 1) * P], wr[:, d, :],
                                         start=(d == 0), stop=(d == DC - 1))
                last.then_inc(done, 1)

            def entry(it):
                for k in range(2):
                    pe.wait_ge(a_xn, it * 2 + k + 1)
                    if later(it):
                        pe.wait_ge(a_xt, 2 * it - 1 + k)
                    turn_rows(xnc[k], bank[2 * k:2 * k + 2], a_t)
                    pe.wait_ge(a_xt, it * 2 + k + 1)
                    if later(it) or k:
                        pe.wait_ge(a_lgsb, it * 2 + k)
                    route_logits(xtc, bank[6][:, k * CT * E:(k + 1) * CT * E], a_lg)
            Chain(pe, None).loop(ENTRY, entry)

            def route(ph):
                s = S[ph]
                onehot = rt[3][:, 0:E * NJ // 2].bitcast(BF16)
                pe.wait_ge(s["onehot"], 1)
                pe.matmul(bank[5][:, 0:256], before[:], onehot, start=True, stop=True)
                pe.matmul(bank[5][:, 256:512], ones[:], onehot, start=True, stop=True).then_inc(s["counts"], 1)
                pe.wait_ge(s["pos"], 1)
                for g in range(NJ // GR):
                    pe.wait_ge(s["row"], g + 1)
                    for i in range(GR):
                        j = GR * g + i
                        last = pe.matmul(bank[4][:, 0:4 * NT], onerow[g % 2][:, i, :],
                                         sval[:, j, :, :].rearrange("p a b -> p (a b)"),
                                         start=(j == 0), stop=(j == NJ - 1))
                    last.then_inc(s["rowused"], 1)
                pe.wait_ge(s["sorted_sb"], 1)

            def ffn(ph):
                s = S[ph]

                def turn_tile(q, k):
                    pe.wait_ge(s["xn"], q + 1)
                    if not isinstance(q, int) or q >= 2:
                        pe.wait_ge(s["xt"], q - 1)
                    for d in range(DC):
                        last = pe.transpose(bank[6 + k % 2][:, d * P:(d + 1) * P], xng[k % 2][:, d * P:(d + 1) * P],
                                            ident[:])
                    last.then_inc(s["turned"], 1)

                def product1(q, k):
                    e = pe.value_load(eid[0:1, at(q, 1)], min_val=0, max_val=E - 1)
                    w = pe.snap(e * (2 * WE))
                    pe.wait_ge(s["xt"], q + 1)
                    for half in range(2):
                        acc = bank[2 * (k % 2) + half]
                        if not isinstance(q, int) or q >= 2:
                            pe.wait_ge(s["gelu"], q * 2 - 3 + half)
                        for f in range(4 * half, 4 * half + 4):
                            n = 0
                            for wpart in range(2):
                                for d in range(DC):
                                    weights = w1s[:, bass.ds(w + (wpart * WE + d * F + f * P), P)]
                                    for xpart in range(2 - wpart):
                                        last = pe.matmul(acc[:, (f % 4) * P:(f % 4 + 1) * P], weights,
                                                         xts[k % 2][:, xpart, d, :], start=(n == 0), stop=(n == 5))
                                        n += 1
                        last.then_inc(s["m1"], 1)

                def product2(q, k):
                    e = pe.value_load(eid[0:1, at(q, 1)], min_val=0, max_val=E - 1)
                    w = pe.snap(e * (2 * WE))
                    acc = bank[4 + k % 2]
                    if not isinstance(q, int) or q >= 2:
                        pe.wait_ge(s["o"], q - 1)
                    for f in range(FC):
                        if f % 4 == 0:
                            pe.wait_ge(s["hsplit"], q * 2 + f // 4 + 1)
                        both = w2s[:, bass.ds(w + f * 2 * D, 2 * D)]
                        hi = w2s[:, bass.ds(w + f * 2 * D, D)]
                        pe.matmul(acc[:], hs[k % 2][:, 0, f, :], both, start=(f == 0), stop=False)
                        last = pe.matmul(acc[:, 0:D], hs[k % 2][:, 1, f, :], hi, start=False, stop=(f == FC - 1))
                    last.then_inc(s["m2"], 1)

                def step(q, k):
                    if not isinstance(q, int) or q + 2 < NT:
                        turn_tile(q + 2, (k + 2) % RING)
                    if not isinstance(q, int) or q + 1 < NT:
                        product1(q + 1, (k + 1) % RING)
                    product2(q, k)

                turn_tile(0, 0)
                turn_tile(1, 1)
                product1(0, 0)
                for q in range(RING):
                    step(q, q % RING)
                with pe.Fori(1, NT // RING - 1) as it:
                    for k in range(RING):
                        step(it * RING + k, k)
                for q in range(NT - RING, NT):
                    step(q, q % RING)

            route(1)
            ffn(1)
            for c in range(NC + 2):
                if c < NC:
                    pe.wait_ge(s_un, c + 1)
                    if c >= 1:
                        pe.wait_ge(s_uts, c)
                    turn_rows(uns[c % 2], bank[0:2], s_ut)
                    pe.wait_ge(s_uts, c + 1)
                    if c >= 1:
                        pe.wait_ge(s_in, c)
                    for d in range(DC):
                        last = pe.matmul(bank[4][:], bt[:, d, :], uts[:, d, :], start=(d == 0), stop=(d == DC - 1))
                    last.then_inc(s_g, 1)
                if 1 <= c <= NC:
                    b = c - 1
                    pe.wait_ge(s_hr, b + 1)
                    if b >= 1:
                        pe.wait_ge(s_x2, b)
                    for i in range(CT):
                        last = pe.matmul(bank[6 + i // 2][:, (i % 2) * D:(i % 2 + 1) * D],
                                         hr[b % 2][:, i * P:(i + 1) * P], ct[:], start=True, stop=True)
                    last.then_inc(s_y, 1)
                if c >= 2:
                    b = c - 2
                    pe.wait_ge(s_xn3, b + 1)
                    if b >= 1:
                        pe.wait_ge(s_xt3, b)
                    turn_rows(xn3[b % 2], bank[2:4], s_t3)
                    pe.wait_ge(s_xt3, b + 1)
                    if b >= 1:
                        pe.wait_ge(s_lgsb, b)
                    route_logits(xt3, bank[5][:, 0:CT * E], s_lg)
            route(2)
            ffn(2)


INPUTS = ("L0_attn_u L0_attn_A_real L0_attn_A_imag L0_attn_B L0_attn_C L0_ffn_Wr L0_ffn_W1 L0_ffn_b1 L0_ffn_W2 "
          "L0_ffn_b2").split()


def kernel(**inputs):
    import concourse.bacc as bacc
    import numpy as np
    from concourse.bass_utils import run_bass_kernel_spmd

    nc = bacc.Bacc("TRN2", target_bir_lowering=False, num_devices=1)
    arrays = {name: np.ascontiguousarray(inputs[name]) for name in INPUTS}
    aps = {name: nc.dram_tensor(name, a.shape, F32, kind="ExternalInput").ap() for name, a in arrays.items()}
    aps["out"] = nc.dram_tensor("out", (1, T, D), F32, kind="ExternalOutput").ap()
    macaron(nc, aps)
    return run_bass_kernel_spmd(nc, [arrays], core_ids=[0]).results[0]["out"]
```

```python
from contextlib import ExitStack

import concourse.bass as bass
from concourse import mybir

F32 = mybir.dt.float32
F16 = mybir.dt.float16
BF16 = mybir.dt.bfloat16
I32 = mybir.dt.int32
U32 = mybir.dt.uint32
U8 = mybir.dt.uint8
ALU = mybir.AluOpType
ACT = mybir.ActivationFunctionType
AX = mybir.AxisListType.X
ABSMAX = bass.bass_isa.ReduceOp.absmax

P = 128
T = 4096
D = 256
DC = D // P
E = 8
F = 1024
FC = F // P
N = 128
NJ = T // P
CH = 512
CT = CH // P
NC = T // CH
NT = NJ + E - 1
GR = 4
RING = 6
EPS = 1e-5
DT = 0.01
BIG = 8192.0
SX = 2.0 ** 10
TOP = 2.0 ** 14
HB = float(D)
EXPONENT = 0x7F800000
TINY = 1e-30
WE = DC * F
WB = 2 * WE * 2
LAG = 4
TURNS = NT // RING
AHEAD = 2


def hold(engine, held, sem, value):
    engine.wait_ge(sem, value)
    if not isinstance(value, int):
        engine.sem_inc(held, 1)


def tile(turn, k):
    turn, k = turn + k // RING, k % RING
    return turn * RING + k, k, turn


def over_tiles(engine, step):
    for k in range(RING):
        step(0, k)
    with engine.Fori(1, TURNS) as it:
        for k in range(RING):
            step(it, k)
    for k in range(NT - TURNS * RING):
        step(TURNS, k)


def chunk(turn, k):
    turn, k = turn + k // 2, k % 2
    return turn * 2 + k, k, turn


def before(q, end):
    return not isinstance(q, int) or q < end


def has(q, n):
    return not isinstance(q, int) or q >= n


class Chain:

    def __init__(self, engine, sem, held=None):
        self.engine, self.sem, self.held = engine, sem, held
        self.n = 0
        self.turns = 0

    def link(self, instruction):
        instruction.then_inc(self.sem, 1)
        self.n += 1
        hold(self.engine, self.held, self.sem, self.turns + self.n)

    def over_chunks(self, step):
        start = self.n
        step(0, 0)
        step(0, 1)
        first = self.n - start
        with self.engine.Fori(1, NC // 2 - 1) as it:
            self.turns, self.n = it * first, start
            step(it, 0)
            step(it, 1)
            assert self.n - start == first
        self.turns, self.n = 0, start + first * (NC // 2 - 1)
        step(NC // 2 - 1, 0)
        step(NC // 2 - 1, 1)


def macaron(nc, A):
    u, out = A["L0_attn_u"][0], A["out"][0]
    x1_dram = nc.dram_tensor("x_after_ffn1", [T, D], F32, kind="Internal").ap()
    x2_dram = nc.dram_tensor("x_after_ssm", [T, D], F32, kind="Internal").ap()
    ctx = ExitStack()
    with ctx:
        def sb(name, shape, dt=F32):
            return ctx.enter_context(nc.sbuf_tensor(name, shape, dt))

        def sem(name):
            return ctx.enter_context(nc.semaphore(name))

        ARENA = 15872
        big = sb("weights_arena", [P, 2 * E * WB + 4 * ARENA], U8)
        iota_r = sb("iota_r", [P, P])
        part = sb("part", [P, 1])
        part_i = sb("part_i", [P, 1], I32)
        iota_i = sb("iota_i", [P, P], I32)
        ident = sb("ident", [P, P])
        earlier = sb("earlier", [P, P], BF16)
        ones = sb("ones", [P, P], BF16)
        one = sb("one", [P, 1])
        rev = sb("rev", [P, E])
        tid = sb("tid", [P, NJ])
        mhalf = sb("mhalf", [P, CT])
        wr = sb("wr", [P, DC, E])
        bt = sb("bt", [P, DC, N])
        ct = sb("ct", [P, D])
        b1t = sb("b1t", [P, E * FC])
        ev = sb("ev", [P, 24])
        turn = sb("turn", [P, 2, CH])
        back = sb("back", [P, 2, CH])
        rho = sb("rho", [P, 1])
        state = sb("state", [P, 2])
        wmax2 = sb("wmax2", [P, 2, 2])
        wall2 = sb("wall2", [P, 2, 2])
        b1max = sb("b1max", [P, E])
        b1all = sb("b1all", [P, E])
        wall = sb("wall", [P, 2 * E])
        wpow = sb("wpow", [P, 2 * E])
        wscale = sb("wscale", [P, 2 * E])
        hpow = sb("hpow", [P, E])
        hscale = sb("hscale", [P, E])
        inv1 = sb("inv1", [P, E])
        inv2 = sb("inv2", [P, E])
        logits = sb("logits", [P, NJ, E])
        nmean = sb("nmean", [P, NJ])
        rstd = sb("rstd", [P, NJ])
        halfp = sb("halfp", [P, NJ])
        sortf = sb("sortf", [P, NT, 3])
        sorti = sb("sorti", [P, NT, 2], I32)
        eid = sb("eid", [P, NT], I32)

        def view(at, *shape, dt=F32):
            size = 1
            for s in shape:
                size *= s
            words = size // 2 if dt is F16 else size
            assert at + words <= ARENA
            a = big[:, 2 * E * WB + 4 * at:2 * E * WB + 4 * (at + words)].bitcast(dt)
            names = "abcd"[:len(shape)]
            if len(shape) == 1:
                return a
            return a.rearrange("p (" + " ".join(names) + ") -> p " + " ".join(names),
                               **{n: s for n, s in zip(names, shape)})

        xc = [view(8192 + k * CT * D, CT, D) for k in range(2)]
        xnc = [view(10240 + k * CT * D, CT, D) for k in range(2)]
        xtc = view(12288, DC, CH)
        sval = view(8192, NJ, 4, NT)
        onerow = [view(13312 + k * GR * P, GR, P) for k in range(2)]
        rt = [view(14336 + 256 * k, E * NJ) for k in range(6)]
        hb = [view(k * 1024, FC, P) for k in range(2)]
        hs = [view(2048 + k * 1024, 2, FC, P, dt=F16) for k in range(2)]
        xg = [view(4096 + k * D, D) for k in range(RING)]
        xng = [view(5632 + k * D, D) for k in range(2)]
        xts = [view(6144 + k * 256, 2, DC, P, dt=F16) for k in range(2)]
        og = [view(6656 + k * D, D) for k in range(2)]
        b2b = view(7168, E * D)
        xs = [view(k * CT * D, CT, D) for k in range(4)]
        uns = [view(4096 + k * CT * D, CT, D) for k in range(2)]
        uts = view(6144, DC, CH)
        xn3 = [view(7168 + k * CT * D, CT, D) for k in range(2)]
        xt3 = view(9216, DC, CH)
        mod = view(10240, 2, CH)
        zz = view(11264, 2, CH)
        aa = view(12288, 2, CH)
        hr = [view(13312 + k * CH, CH) for k in range(2)]

        recf = sb("recf", [P, RING, 3])
        gidx = sb("gidx", [P, RING], I32)
        sidx = sb("sidx", [P, RING], I32)
        stats = sb("stats", [P, 4, CT, 6])
        mv = sb("mv", [P, 4, CT, 2])
        ve = sb("ve", [P, 4, CT])
        nm = sb("nm", [P, 2, CT])
        rs = sb("rs", [P, 2, CT])
        nb = sb("nb", [P, 4, CT])

        bank = [ctx.enter_context(nc.psum_tensor(f"bank{k}", [P, 512], F32)) for k in range(8)]

        par_in = sem("par_in")
        xload = [sem(f"xload{k}") for k in range(2)]
        wload = [sem(f"wload{k}") for k in range(4)]
        iota_done = sem("iota_done")
        const_done = sem("const_done")
        par_t = sem("par_t")
        par_sb = sem("par_sb")
        dve_chain = sem("dve_chain")
        pool_chain = sem("pool_chain")
        pool_held, act_held, dve_held = sem("pool_held"), sem("act_held"), sem("dve_held")
        rho_in = sem("rho_in")
        rho_out = sem("rho_out")
        a_stats = sem("a_stats")
        a_nb = sem("a_nb")
        s_nb = sem("s_nb")
        s_nb3 = sem("s_nb3")
        a_xn = sem("a_xn")
        a_t = sem("a_t")
        a_xt = sem("a_xt")
        a_lg = sem("a_lg")
        a_lgsb = sem("a_lgsb")
        w_max = sem("w_max")
        w_all = sem("w_all")
        w_sc = sem("w_sc")
        w_hi = sem("w_hi")
        w_ws = sem("w_ws")
        w_lo = sem("w_lo")
        b1_max = sem("b1_max")
        b1_all = sem("b1_all")
        inv_done = sem("inv_done")
        S = {}
        for ph in (1, 2):
            S[ph] = {k: sem(f"{k}_{ph}") for k in (
                "diff exps onehot counts pos row rowused sorted_sb b2in rec sidx xn turned "
                "xt_hi xt m1 gelu h_hi hsplit m2 o_chain o").split()}
            S[ph]["gath"] = [sem(f"gath{k}_{ph}") for k in range(RING)]
            S[ph]["scat"] = [sem(f"scat{k}_{ph}") for k in range(RING)]
        sx = [sem(f"s_load{k}") for k in range(4)]
        s_store = [sem(f"s_store{k}") for k in range(4)]
        s_stats, s_un, s_ut, s_uts, s_g, s_in, s_hr, s_y, s_x2, s_st3, s_xn3, s_t3, s_xt3, s_lg, s_lgsb = (
            sem(n) for n in ("s_stats s_un s_ut s_uts s_g s_in s_hr s_y s_x2 s_st3 s_xn3 s_t3 s_xt3 s_lg "
                             "s_lgsb").split())

        W1 = A["L0_ffn_W1"].rearrange("e (c p) f -> e p c f", p=P)
        W2 = A["L0_ffn_W2"].rearrange("e (c p) d -> e p c d", p=P)
        u_chunks = u.rearrange("(n i p) d -> n p i d", p=P, i=CT)
        x1_chunks = x1_dram.rearrange("(n i p) d -> n p i d", p=P, i=CT)
        x2_chunks = x2_dram.rearrange("(n i p) d -> n p i d", p=P, i=CT)
        ENTRY = NC // 2

        def in_slot(k):
            return len(range(k, NT, RING))

        def later(it):
            return not (isinstance(it, int) and it == 0)

        def at(q, n):
            return bass.ds(q * n, n)

        def weight_parts(e, which):
            a = big[:, bass.ds(e * (2 * WB) + which * WB, WB)].bitcast(F16)
            if which == 0:
                a = a.rearrange("p (h w) -> p h w", h=2)
            else:
                a = a.rearrange("p (f h d) -> p h f d", f=FC, h=2)
            return a[:, 0], a[:, 1]

        def raw(e, which):
            a = big[:, bass.ds(e * (2 * WB) + (which + LAG) * WB, WB)].bitcast(F32)
            return a if which == 0 else a.rearrange("p (f d) -> p f d", f=FC)

        braw = view(14336, D)
        craw = view(14592, DC, N)
        b1raw = view(14848, P)[0:E * FC]
        araw = sb("araw", [P, 2])
        NPAR = 6
        block = ctx.enter_context(nc.Block())

        @block.sync
        def _(sp):
            sp.dma_start(araw[:, 0:1], A["L0_attn_A_real"].unsqueeze(1)).then_inc(par_in, 16)
            sp.dma_start(araw[:, 1:2], A["L0_attn_A_imag"].unsqueeze(1)).then_inc(par_in, 16)
            sp.dma_start(braw, A["L0_attn_B"]).then_inc(par_in, 16)
            sp.dma_start(craw, A["L0_attn_C"].rearrange("(c p) n -> p c n", p=P)).then_inc(par_in, 16)
            sp.dma_start(wr[:], A["L0_ffn_Wr"].rearrange("(c p) e -> p c e", p=P)).then_inc(par_in, 16)
            sp.dma_start(b1raw, A["L0_ffn_b1"].rearrange("e (c p) -> (e c) p", p=P)).then_inc(par_in, 16)

            def load_x(turn, k):
                c, k, turn = chunk(turn, k)
                if has(c, 2):
                    sp.wait_ge(a_xn, c - 1)
                sp.dma_start(xc[k], u_chunks[bass.ds(c, 1)].squeeze(0)).then_inc(xload[k], 16)

            def load_weights(turn, k):
                e, k, turn = chunk(turn, k)
                for which, W in enumerate((W1, W2)):
                    sp.dma_start(big[:, bass.ds(e * (2 * WB) + (which + LAG) * WB, WB)].bitcast(F32)
                                 .rearrange("p (c f) -> p c f", c=W.shape[2]),
                                 W[bass.ds(e, 1)].squeeze(0)).then_inc(wload[2 * k + which], 16)

            def entry(turn, k):
                c = chunk(turn, k)[0]
                if before(c, NC - 1):
                    load_weights(turn, k + 1)
                if before(c, NC - 2):
                    load_x(turn, k + 2)
            load_x(0, 0)
            load_weights(0, 0)
            load_x(0, 1)
            Chain(sp, None).over_chunks(entry)

            def load_b2(ph):
                sp.wait_ge(S[ph]["sorted_sb"], 1)
                if ph == 1:
                    sp.wait_ge(w_lo, 2 * E)
                sp.dma_start(b2b, A["L0_ffn_b2"].rearrange("e d -> (e d)").partition_broadcast(P)) \
                    .then_inc(S[ph]["b2in"], 16)
            load_b2(1)
            for k in range(RING):
                sp.wait_ge(S[1]["scat"][k], 16 * in_slot(k))
            for c in range(NC):
                if c >= 4:
                    sp.wait_ge(s_store[c % 4], 16 * (c // 4))
                    sp.wait_ge(s_xn3, c - 3)
                sp.dma_start(xs[c % 4], x1_chunks[c]).then_inc(sx[c % 4], 16)
                if c >= 3:
                    sp.wait_ge(s_x2, c - 2)
                    sp.dma_start(x2_chunks[c - 3], xs[(c - 3) % 4]).then_inc(s_store[(c - 3) % 4], 16)
            for c in range(NC - 3, NC):
                sp.wait_ge(s_x2, c + 1)
                sp.dma_start(x2_chunks[c], xs[c % 4]).then_inc(s_store[c % 4], 16)
            load_b2(2)
            for k in range(RING):
                sp.wait_ge(S[2]["scat"][k], 16 * in_slot(k))

        @block.gpsimd
        def _(pool):
            chain = Chain(pool, pool_chain, pool_held)
            pool.iota(iota_i[:], [[1, P]], base=0, channel_multiplier=0).then_inc(iota_done, 1)
            pool.iota(part_i[:], [[0, 1]], base=0, channel_multiplier=1).then_inc(iota_done, 1)
            pool.memset(mhalf[:], -0.5).then_inc(iota_done, 1)
            hold(pool, pool_held, iota_done, 3)

            def inv_std(slot, means, to, ready, n, done):
                hold(pool, pool_held, ready, n)
                chain.link(pool.tensor_tensor(to, ve[:, slot, :], mhalf[:], ALU.pow))
                pool.tensor_tensor(nb[:, slot, :], means, to, ALU.mult).then_inc(done, 1)

            def entry_std(turn, k):
                c, k, turn = chunk(turn, k)
                if has(c, 2):
                    hold(pool, pool_held, a_xn, c - 1)
                inv_std(k, nmean[:, at(c, CT)], rstd[:, at(c, CT)], a_stats, c + 1, a_nb)

            def low_parts(turn, k):
                e, k, turn = chunk(turn, k)
                for which in range(2):
                    hi, lo = weight_parts(e, which)
                    hold(pool, pool_held, w_ws, 2 * e + which + 1)
                    pool.tensor_tensor(lo, raw(e, which), hi, ALU.subtract).then_inc(w_lo, 1)

            def entry(turn, k):
                c = chunk(turn, k)[0]
                if before(c, NC - 1):
                    entry_std(turn, k + 1)
                hold(pool, pool_held, w_max, 2 * c + 2)
                pool.partition_all_reduce(wall2[:, k, :], wmax2[:, k, :], P, ABSMAX).then_inc(w_all, 1)
                if has(c, 1):
                    low_parts(turn, k - 1)
            entry_std(0, 0)
            chain.over_chunks(entry)
            hold(pool, pool_held, b1_max, 1)
            pool.partition_all_reduce(b1all[:], b1max[:], P, ABSMAX).then_inc(b1_all, 1)
            low_parts(NC // 2 - 1, 1)

            def ffn(ph, src, dst):
                s = S[ph]
                table = src
                hold(pool, pool_held, s["sorted_sb"], 1)
                if ph == 2:
                    for k in range(4):
                        hold(pool, pool_held, s_store[k], 16 * (NC // 4))
                else:
                    hold(pool, pool_held, w_lo, 2 * E)

                def fetch(turn, k):
                    q, k, turn = tile(turn, k)
                    if has(q, RING):
                        hold(pool, pool_held, s["o"], q - RING + 1)
                    pool.tensor_copy(recf[:, k, :], sortf[:, at(q, 1), :].squeeze(1)).then_inc(s["rec"], 1)
                    pool.tensor_copy(gidx[:, k:k + 1], sorti[:, at(q, 1), 0:1].squeeze(1)).then_inc(s["rec"], 1)
                    hold(pool, pool_held, s["rec"], 2 * q + 2)
                    pool.indirect_dma_start(xg[k], None, table, bass.IndirectOffsetOnAxis(ap=gidx[:, k:k + 1].bitcast(U32), axis=0)) \
                        .then_inc(s["gath"][k], 16)

                def norm(turn, k):
                    q, k, turn = tile(turn, k)
                    if has(q, 2):
                        hold(pool, pool_held, s["turned"], q - 1)
                    hold(pool, pool_held, s["gath"][k], turn * 16 + 16)
                    pool.tensor_scalar(xng[k % 2], xg[k], recf[:, k, 0:1], recf[:, k, 1:2], ALU.add, ALU.mult) \
                        .then_inc(s["xn"], 1)

                def scatter(turn, k):
                    q, k, turn = tile(turn, k)
                    hold(pool, pool_held, s["o"], q + 1)
                    pool.tensor_copy(sidx[:, k:k + 1], sorti[:, at(q, 1), 1:2].squeeze(1)).then_inc(s["sidx"], 1)
                    hold(pool, pool_held, s["sidx"], q + 1)
                    pool.indirect_dma_start(dst, bass.IndirectOffsetOnAxis(ap=sidx[:, k:k + 1].bitcast(U32), axis=0),
                                            og[k % 2], None, bounds_check=T - 1, oob_is_err=False) \
                        .then_inc(s["scat"][k], 16)

                def step(turn, k):
                    q = tile(turn, k)[0]
                    if has(q, AHEAD):
                        norm(turn, k - AHEAD)
                    if has(q, RING):
                        scatter(turn, k - RING)
                    fetch(turn, k)

                over_tiles(pool, step)
                left = NT - TURNS * RING
                for k in range(left - AHEAD, left):
                    norm(TURNS, k)
                for k in range(left - RING, left):
                    scatter(TURNS, k)

            ffn(1, u, x1_dram)
            hold(pool, pool_held, rho_in, 1)
            pool.tensor_tensor(ev[:, 13:14], ev[:, 12:13], mhalf[:, 0:1], ALU.pow).then_inc(rho_out, 1)
            for c in range(NC + 2):
                if c < NC:
                    if c >= 2:
                        hold(pool, pool_held, s_un, c - 1)
                    inv_std(c % 2, nm[:, c % 2, :], rs[:, c % 2, :], s_stats, c + 1, s_nb)
                if c >= 2:
                    d = c - 2
                    if d >= 2:
                        hold(pool, pool_held, s_xn3, d - 1)
                    inv_std(2 + d % 2, nmean[:, d * CT:(d + 1) * CT], rstd[:, d * CT:(d + 1) * CT], s_st3, d + 1, s_nb3)
            ffn(2, x2_dram, out)

        @block.scalar
        def _(act):
            def normalise(slot, src, dst, scales, ready, n, done):
                hold(act, act_held, ready, n)
                for i in range(CT):
                    last = act.activation(dst[:, i, :], src[:, i, :], ACT.Identity, bias=nb[:, slot, i:i + 1],
                                          scale=scales(i))
                last.then_inc(done, 1)

            def entry_rows(turn, k):
                c, k, turn = chunk(turn, k)
                if has(c, 2):
                    hold(act, act_held, a_t, c - 1)
                normalise(k, xc[k], xnc[k], lambda i: rstd[:, bass.ds(c * CT + i, 1)], a_nb, c + 1, a_xn)

            def entry(turn, k):
                c = chunk(turn, k)[0]
                if before(c, NC - 1):
                    entry_rows(turn, k + 1)
                hold(act, act_held, a_t, c + 1)
                if has(c, 1):
                    hold(act, act_held, a_lg, c)
                for d in range(DC):
                    last = act.copy(xtc[:, d, :], bank[2 * k + d][:])
                last.then_inc(a_xt, 1)
                hold(act, act_held, w_sc, c + 1)
                for which in range(2):
                    hi, lo = weight_parts(c, which)
                    src = raw(c, which)
                    scale = wscale[:, bass.ds(c * 2 + which, 1)]
                    if has(c, 2):
                        hold(act, act_held, w_lo, 2 * c + which - LAG + 1)
                    act.activation(hi, src, ACT.Copy, scale=scale).then_inc(w_hi, 1)
                    hold(act, act_held, w_hi, 2 * c + which + 1)
                    act.activation(src, src, ACT.Copy, scale=scale).then_inc(w_ws, 1)
            entry_rows(0, 0)
            Chain(act, None).over_chunks(entry)

            def ffn(ph):
                s = S[ph]
                act.wait_ge(s["diff"], 1)
                act.activation(rt[1], rt[0], ACT.Exp).then_inc(s["exps"], 1)
                act.wait_ge(s["sorted_sb"], 1)
                act.wait_ge(inv_done, 1)

                def step(turn, k):
                    q, k, turn = tile(turn, k)
                    e = act.value_load(eid[0:1, at(q, 1)], min_val=0, max_val=E - 1)
                    for half in range(2):
                        act.wait_ge(s["m1"], q * 2 + half + 1)
                        if half == 0 and (not isinstance(q, int) or q >= 2):
                            act.wait_ge(s["hsplit"], q * 2 - 2)
                        for f in range(half * 4, half * 4 + 4):
                            src = bank[2 * (k % 2) + half][:, (f % 4) * P:(f % 4 + 1) * P]
                            last = act.activation(hb[k % 2][:, f, :], src, ACT.Gelu,
                                                  bias=b1t[:, bass.ds(e * FC + f, 1)], scale=inv1[:, bass.ds(e, 1)])
                        last.then_inc(s["gelu"], 1)

                over_tiles(act, step)
            ffn(1)
            for c in range(NC + 2):
                if c < NC:
                    if c >= 2:
                        act.wait_ge(s_ut, c - 1)
                    normalise(c % 2, xs[c % 4], uns[c % 2], lambda i: rs[:, c % 2, i:i + 1], s_nb, c + 1, s_un)
                    act.wait_ge(s_ut, c + 1)
                    if c >= 1:
                        act.wait_ge(s_g, c)
                    for d in range(DC):
                        last = act.copy(uts[:, d, :], bank[d][:])
                    last.then_inc(s_uts, 1)
                if c >= 2:
                    d3 = c - 2
                    if d3 >= 2:
                        act.wait_ge(s_t3, d3 - 1)
                    normalise(2 + d3 % 2, xs[d3 % 4], xn3[d3 % 2], lambda i: rstd[:, d3 * CT + i:d3 * CT + i + 1],
                              s_nb3, d3 + 1, s_xn3)
                    act.wait_ge(s_t3, d3 + 1)
                    if d3 >= 1:
                        act.wait_ge(s_lg, d3)
                    for d in range(DC):
                        last = act.copy(xt3[:, d, :], bank[2 + d][:])
                    last.then_inc(s_xt3, 1)
            ffn(2)

        @block.vector
        def _(dve):
            chain = Chain(dve, dve_chain, dve_held)
            link = chain.link
            dve.wait_ge(iota_done, 2)
            dve.tensor_copy(iota_r[:], iota_i[:])
            link(dve.tensor_copy(part[:], part_i[:]))
            dve.tensor_scalar(ident[:], iota_r[:], part[:], None, ALU.is_equal).then_inc(const_done, 1)
            dve.tensor_scalar(earlier[:], iota_r[:], part[:], None, ALU.is_gt)
            dve.memset(ones[:], 1.0)
            dve.memset(one[:], 1.0)
            dve.tensor_scalar(rev[:], iota_r[:, 0:E], -1.0, float(E), ALU.mult, ALU.add)
            link(dve.tensor_scalar(tid[:], iota_r[:, 0:NJ], float(P), -BIG, ALU.mult, ALU.add))
            dve.tensor_scalar(tid[:], tid[:], part[:], None, ALU.add)

            dve.wait_ge(par_t, 1)
            dve.tensor_copy(bt[:], bank[4][:, 0:DC * N].rearrange("p (c n) -> p c n", c=DC))
            dve.tensor_copy(ct[:], bank[4][:, DC * N:DC * N + D]).then_inc(par_sb, 1)
            link(dve.tensor_copy(b1t[:], bank[5][:, 0:E * FC]))
            dve.tensor_reduce(b1max[:], b1t[:].rearrange("p (e c) -> p e c", c=FC), AX, ALU.max,
                              apply_absolute_value=True).then_inc(b1_max, 1)

            def row_stats(src, k, means, done):
                for i in range(CT):
                    last = dve.bn_stats(stats[:, k, i, :], src[:, i, :])
                link(last)
                for i in range(CT):
                    last = dve.bn_aggr(mv[:, k, i, :], stats[:, k, i, :])
                link(last)
                dve.tensor_scalar(means, mv[:, k, :, 0], -1.0, None, ALU.mult)
                dve.tensor_scalar(ve[:, k, :], mv[:, k, :, 1], EPS, None, ALU.add).then_inc(done, 1)

            def entry_stats(turn, k):
                c, k, turn = chunk(turn, k)
                dve.wait_ge(xload[k], turn * 16 + 16)
                if has(c, 2):
                    dve.wait_ge(a_nb, c - 1)
                row_stats(xc[k], k, nmean[:, at(c, CT)], a_stats)

            def entry_logits(turn, k):
                c, k, turn = chunk(turn, k)
                dve.wait_ge(a_lg, c + 1)
                dve.tensor_copy(logits[:, at(c, CT), :],
                                bank[6 + k][:, 0:CT * E].rearrange("p (i e) -> p i e", e=E)).then_inc(a_lgsb, 1)

            def entry(turn, k):
                c = chunk(turn, k)[0]
                if before(c, NC - 1):
                    entry_stats(turn, k + 1)
                for which in range(2):
                    dve.wait_ge(wload[2 * k + which], turn * 16 + 16)
                    dve.tensor_reduce(wmax2[:, k, which:which + 1],
                                      big[:, bass.ds(c * (2 * WB) + (which + LAG) * WB, WB)].bitcast(F32),
                                      AX, ALU.max, apply_absolute_value=True).then_inc(w_max, 1)
                if has(c, 1):
                    entry_logits(turn, k - 1)
                two = at(c, 2)
                dve.wait_ge(w_all, c + 1)
                link(dve.tensor_scalar(wall[:, two], wall2[:, k, :], TINY, None, ALU.max))
                link(dve.tensor_scalar(wpow[:, two].bitcast(I32), wall[:, two].bitcast(I32), EXPONENT, None,
                                       ALU.bitwise_and))
                link(dve.reciprocal(wscale[:, two], wpow[:, two]))
                dve.tensor_scalar(wscale[:, two], wscale[:, two], TOP, None, ALU.mult).then_inc(w_sc, 1)
            entry_stats(0, 0)
            chain.over_chunks(entry)
            entry_logits(NC // 2 - 1, 1)
            dve.wait_ge(a_lgsb, NC)

            def product_scales():
                dve.wait_ge(b1_all, 1)
                w2x = lambda t, k: t[:, 0:2 * E].rearrange("p (e k) -> p k e", k=2)[:, k, :]
                link(dve.scalar_tensor_tensor(hpow[:], w2x(wall, 0), HB, b1all[:], ALU.mult, ALU.add))
                link(dve.tensor_scalar(hpow[:].bitcast(I32), hpow[:].bitcast(I32), EXPONENT, None, ALU.bitwise_and))
                link(dve.reciprocal(hscale[:], hpow[:]))
                dve.tensor_scalar(hscale[:], hscale[:], TOP, None, ALU.mult)
                dve.tensor_scalar(inv1[:], w2x(wpow, 0), 1.0 / (TOP * SX), None, ALU.mult)
                link(dve.tensor_scalar(hpow[:], hpow[:], 1.0 / TOP, None, ALU.mult))
                dve.scalar_tensor_tensor(inv2[:], w2x(wpow, 1), 1.0 / TOP, hpow[:], ALU.mult, ALU.mult) \
                    .then_inc(inv_done, 1)

            def route(ph):
                s = S[ph]
                je = lambda a: a.rearrange("p (j e) -> p j e", e=E)
                ej = lambda a: a.rearrange("p (e j) -> p e j", e=E)
                swap = lambda a: a.rearrange("p (e j) -> p j e", e=E)
                over_e = lambda a: a.unsqueeze(2).to_broadcast([P, NJ, E])
                top = rt[5][:, 0:NJ]
                first = rt[5][:, NJ:2 * NJ]
                pos = rt[5][:, 2 * NJ:3 * NJ]
                tile = rt[5][:, 3 * NJ:4 * NJ]
                slot = rt[5][:, 4 * NJ:5 * NJ]
                small = lambda k: rt[5][:, 5 * NJ + 8 * k:5 * NJ + 8 * k + 8]
                link(dve.tensor_reduce(top, logits[:], AX, ALU.max))
                dve.tensor_tensor(je(rt[0]), logits[:], over_e(top), ALU.subtract).then_inc(s["diff"], 1)
                link(dve.tensor_tensor(je(rt[2]), logits[:], over_e(top), ALU.is_equal))
                link(dve.tensor_tensor(je(rt[2]), je(rt[2]), rev[:].unsqueeze(1).to_broadcast([P, NJ, E]), ALU.mult))
                link(dve.tensor_reduce(first, je(rt[2]), AX, ALU.max))
                onehot = rt[3][:, 0:E * NJ // 2].bitcast(BF16)
                dve.tensor_tensor(swap(onehot), rev[:].unsqueeze(1).to_broadcast([P, NJ, E]), over_e(first),
                                  ALU.is_equal).then_inc(s["onehot"], 1)
                if ph == 1:
                    product_scales()
                dve.wait_ge(s["exps"], 1)
                link(dve.tensor_reduce(halfp[:], je(rt[1]), AX, ALU.add))
                link(dve.reciprocal(halfp[:], halfp[:]))
                dve.tensor_scalar(halfp[:], halfp[:], 0.5, None, ALU.mult)
                dve.wait_ge(s["counts"], 1)
                link(dve.tensor_copy(rt[2], bank[5][:, 256:512]))
                link(dve.tensor_tensor_scan(rt[4], one[:].to_broadcast([P, E * NJ]), rt[2], 0.0, ALU.mult, ALU.add))
                dve.tensor_tensor(rt[2], rt[4], rt[2], ALU.subtract)
                ends = ej(rt[4])[:, :, NJ - 1]
                cnt, tiles, tend, shift = small(0), small(1), small(2), small(3)
                dve.tensor_tensor(cnt[:, 1:E], ends[:, 1:E], ends[:, 0:E - 1], ALU.subtract)
                link(dve.tensor_copy(cnt[:, 0:1], ends[:, 0:1]))
                link(dve.tensor_scalar(tiles.bitcast(I32), cnt, float(P - 1), None, ALU.add))
                link(dve.tensor_scalar(tend.bitcast(I32), tiles.bitcast(I32), 7, None, ALU.arith_shift_right))
                link(dve.tensor_copy(tiles, tend.bitcast(I32)))
                link(dve.tensor_tensor_scan(tend, one[:].to_broadcast([P, E]), tiles, 0.0, ALU.mult, ALU.add))
                link(dve.tensor_tensor(tiles, tend, tiles, ALU.subtract))
                link(dve.tensor_tensor(cnt, ends, cnt, ALU.subtract))
                link(dve.scalar_tensor_tensor(shift, tiles, float(P), cnt, ALU.mult, ALU.subtract))
                link(dve.tensor_tensor(rt[2], rt[2], bank[5][:, 0:256], ALU.add))
                link(dve.tensor_tensor(ej(rt[2]), ej(rt[2]), shift.unsqueeze(2).to_broadcast([P, E, NJ]), ALU.add))
                link(dve.tensor_tensor(rt[2], rt[2], onehot, ALU.mult))
                link(dve.tensor_reduce(pos, swap(rt[2]), AX, ALU.add))
                posi = tile.bitcast(I32)
                link(dve.tensor_copy(posi, pos))
                sloti = pos.bitcast(I32)
                link(dve.tensor_scalar(sloti, posi, P - 1, None, ALU.bitwise_and))
                tli = first.bitcast(I32)
                link(dve.tensor_scalar(tli, posi, 7, None, ALU.arith_shift_right))
                dve.tensor_copy(slot, sloti)
                link(dve.tensor_copy(tile, tli))
                ntc = sval[:, 0:2, :, :].rearrange("p a b c -> p (a b c)")[:, 0:NT * E].rearrange("p (q e) -> p q e", e=E)
                link(dve.tensor_tensor(ntc, iota_r[:, 0:NT].unsqueeze(2).to_broadcast([P, NT, E]),
                                       tend.unsqueeze(1).to_broadcast([P, NT, E]), ALU.is_ge))
                eidf = rt[5][:, 5 * NJ + 32:5 * NJ + 32 + NT]
                link(dve.tensor_reduce(eidf, ntc, AX, ALU.add))
                dve.tensor_scalar(eid[:], eidf, float(E - 1), None, ALU.min)
                q1 = sval[:, :, 3, :]
                link(dve.tensor_tensor(q1, iota_r[:, 0:NT].unsqueeze(1).to_broadcast([P, NJ, NT]),
                                       tile.unsqueeze(2).to_broadcast([P, NJ, NT]), ALU.is_equal))
                for k, v in enumerate((tid, nmean, rstd, halfp)):
                    last = dve.tensor_tensor(sval[:, :, k, :], q1, v[:].unsqueeze(2).to_broadcast([P, NJ, NT]), ALU.mult)
                last.then_inc(s["pos"], 1)
                for g in range(NJ // GR):
                    if g >= 2:
                        dve.wait_ge(s["rowused"], g - 1)
                    dve.tensor_tensor(onerow[g % 2], iota_r[:].unsqueeze(1).to_broadcast([P, GR, P]),
                                      slot[:, GR * g:GR * g + GR].unsqueeze(2).to_broadcast([P, GR, P]),
                                      ALU.is_equal).then_inc(s["row"], 1)
                dve.wait_ge(s["rowused"], NJ // GR)
                sp4 = bank[4][:, 0:4 * NT].rearrange("p (k q) -> p k q", k=4)
                dve.tensor_scalar(sorti[:, :, 0], sp4[:, 0, :], BIG, float(T - 1), ALU.add, ALU.min)
                dve.tensor_scalar(sorti[:, :, 1], sp4[:, 0, :], BIG, None, ALU.add)
                dve.tensor_copy(sortf[:].rearrange("p q k -> p k q"), sp4[:, 1:4, :]).then_inc(s["sorted_sb"], 1)

            def ffn(ph):
                s = S[ph]
                dve.wait_ge(s["sorted_sb"], 1)
                dve.wait_ge(s["b2in"], 16)

                def expert(q):
                    return dve.value_load(eid[0:1, at(q, 1)], min_val=0, max_val=E - 1)

                def split_x(turn, k):
                    q, k, turn = tile(turn, k)
                    dve.wait_ge(s["turned"], q + 1)
                    if has(q, 2):
                        dve.wait_ge(s["m1"], q * 2 - 2)
                    src = bank[6 + k % 2][:, 0:DC * P].rearrange("p (c t) -> p c t", c=DC)
                    dve.tensor_scalar(xts[k % 2][:, 0], src, SX, None, ALU.mult).then_inc(s["xt_hi"], 1)
                    dve.wait_ge(s["xt_hi"], q + 1)
                    dve.scalar_tensor_tensor(xts[k % 2][:, 1], src, SX, xts[k % 2][:, 0], ALU.mult, ALU.subtract) \
                        .then_inc(s["xt"], 1)

                def split_h(turn, k):
                    q, k, turn = tile(turn, k)
                    e = expert(q)
                    if has(q, 2):
                        dve.wait_ge(s["m2"], q - 1)
                    for half in range(2):
                        f = slice(4 * half, 4 * half + 4)
                        dve.wait_ge(s["gelu"], q * 2 + half + 1)
                        sc = hscale[:, bass.ds(e, 1)]
                        dve.tensor_scalar(hs[k % 2][:, 0, f, :], hb[k % 2][:, f, :], sc, None, ALU.mult) \
                            .then_inc(s["h_hi"], 1)
                        dve.wait_ge(s["h_hi"], q * 2 + half + 1)
                        dve.scalar_tensor_tensor(hs[k % 2][:, 1, f, :], hb[k % 2][:, f, :], sc,
                                                 hs[k % 2][:, 0, f, :], ALU.mult, ALU.subtract).then_inc(s["hsplit"], 1)

                def result(turn, k):
                    _, before_k, before_turn = tile(turn, k - 2)
                    q, k, turn = tile(turn, k)
                    e = expert(q)
                    dve.wait_ge(s["m2"], q + 1)
                    if has(q, 2):
                        dve.wait_ge(s["scat"][before_k], before_turn * 16 + 16)
                    o, acc = og[k % 2], bank[4 + k % 2]
                    i2 = inv2[:, bass.ds(e, 1)]
                    dve.scalar_tensor_tensor(o, acc[:, D:2 * D], i2, b2b[:, bass.ds(e * D, D)], ALU.mult, ALU.add) \
                        .then_inc(s["o_chain"], 1)
                    dve.wait_ge(s["o_chain"], q * 2 + 1)
                    dve.scalar_tensor_tensor(o, acc[:, 0:D], i2, o, ALU.mult, ALU.add).then_inc(s["o_chain"], 1)
                    dve.wait_ge(s["o_chain"], q * 2 + 2)
                    dve.scalar_tensor_tensor(o, o, recf[:, k, 2:3], xg[k], ALU.mult, ALU.add).then_inc(s["o"], 1)

                def step(turn, k):
                    q = tile(turn, k)[0]
                    if not isinstance(q, int) or q + 2 < NT:
                        split_x(turn, k + 2)
                    if not isinstance(q, int) or q + 1 < NT:
                        split_h(turn, k + 1)
                    result(turn, k)

                split_x(0, 0)
                split_x(0, 1)
                split_h(0, 0)
                over_tiles(dve, step)

            route(1)
            ffn(1)

            col = lambda k: ev[:, k:k + 1]
            link(dve.tensor_scalar(ev[:, 0:2], araw[:], DT / 2, None, ALU.mult))
            dve.tensor_scalar(col(2), col(0), -1.0, 1.0, ALU.mult, ALU.add)
            dve.tensor_scalar(col(3), col(0), 1.0, None, ALU.add)
            link(dve.tensor_tensor(col(4), col(1), col(1), ALU.mult))
            dve.scalar_tensor_tensor(col(5), col(2), col(2), col(4), ALU.mult, ALU.add)
            link(dve.scalar_tensor_tensor(col(6), col(3), col(2), col(4), ALU.mult, ALU.subtract))
            dve.reciprocal(col(7), col(5))
            link(dve.tensor_tensor(col(8), col(2), col(3), ALU.add))
            link(dve.tensor_tensor(col(9), col(8), col(1), ALU.mult))
            dve.tensor_tensor(col(10), col(6), col(7), ALU.mult)
            link(dve.tensor_tensor(col(11), col(9), col(7), ALU.mult))
            dve.tensor_scalar(col(14), col(2), col(7), DT ** 0.5, ALU.mult, ALU.mult)
            dve.tensor_scalar(col(15), col(1), col(7), DT ** 0.5, ALU.mult, ALU.mult)
            link(dve.tensor_tensor(col(16), col(10), col(10), ALU.mult))
            dve.scalar_tensor_tensor(col(12), col(11), col(11), col(16), ALU.mult, ALU.add).then_inc(rho_in, 1)
            dve.wait_ge(rho_in, 1)
            dve.wait_ge(rho_out, 1)
            dve.tensor_tensor(rho[:], col(12), col(13), ALU.mult)
            dve.tensor_scalar(turn[:, 0, 0:1], col(10), col(13), None, ALU.mult)
            link(dve.tensor_scalar(turn[:, 1, 0:1], col(11), col(13), None, ALU.mult))
            n = 1
            while n < CH:
                c0, s0 = turn[:, 0, 0:n], turn[:, 1, 0:n]
                cn, sn = turn[:, 0, n - 1:n], turn[:, 1, n - 1:n]
                dve.tensor_scalar(back[:, 0, 0:n], s0, sn, None, ALU.mult)
                link(dve.tensor_scalar(back[:, 1, 0:n], c0, sn, None, ALU.mult))
                dve.scalar_tensor_tensor(turn[:, 0, n:2 * n], c0, cn, back[:, 0, 0:n], ALU.mult, ALU.subtract)
                link(dve.scalar_tensor_tensor(turn[:, 1, n:2 * n], s0, cn, back[:, 1, 0:n], ALU.mult, ALU.add))
                n *= 2
            tmp = aa
            dve.tensor_scalar(tmp[:, 0, :], turn[:, 1, :], col(15), None, ALU.mult)
            link(dve.tensor_scalar(tmp[:, 1, :], turn[:, 0, :], col(15), None, ALU.mult))
            dve.scalar_tensor_tensor(back[:, 0, :], turn[:, 0, :], col(14), tmp[:, 0, :], ALU.mult, ALU.subtract)
            dve.scalar_tensor_tensor(back[:, 1, :], turn[:, 1, :], col(14), tmp[:, 1, :], ALU.mult, ALU.add)
            link(dve.memset(state[:], 0.0))
            for c in range(NC + 3):
                if c < NC:
                    dve.wait_ge(sx[c % 4], 16 * (c // 4) + 16)
                    if c >= 2:
                        dve.wait_ge(s_nb, c - 1)
                    row_stats(xs[c % 4], c % 2, nm[:, c % 2, :], s_stats)
                if 1 <= c <= NC:
                    b = c - 1
                    g = bank[4]
                    dve.wait_ge(s_g, b + 1)
                    dve.tensor_tensor(mod[:, 0, :], g[:], turn[:, 0, :], ALU.mult)
                    dve.scalar_tensor_tensor(mod[:, 1, :], g[:], -1.0, turn[:, 1, :], ALU.mult, ALU.mult) \
                        .then_inc(s_in, 1)
                    dve.wait_ge(s_in, b + 1)
                    dve.tensor_tensor_scan(zz[:, 0, :], rho[:].to_broadcast([P, CH]), mod[:, 0, :], state[:, 0:1],
                                           ALU.mult, ALU.add)
                    link(dve.tensor_tensor_scan(zz[:, 1, :], rho[:].to_broadcast([P, CH]), mod[:, 1, :],
                                                state[:, 1:2], ALU.mult, ALU.add))
                    zr, zi = zz[:, 0, CH - 1:CH], zz[:, 1, CH - 1:CH]
                    cl, sl = turn[:, 0, CH - 1:CH], turn[:, 1, CH - 1:CH]
                    dve.tensor_tensor(ev[:, 20:21], zi, sl, ALU.mult)
                    dve.tensor_tensor(ev[:, 21:22], zr, sl, ALU.mult)
                    dve.tensor_tensor(aa[:, 0, :], zz[:, 0, :], back[:, 0, :], ALU.mult)
                    link(dve.tensor_tensor(aa[:, 1, :], zz[:, 1, :], back[:, 1, :], ALU.mult))
                    dve.scalar_tensor_tensor(state[:, 0:1], zr, cl, ev[:, 20:21], ALU.mult, ALU.subtract)
                    dve.scalar_tensor_tensor(state[:, 1:2], zi, cl, ev[:, 21:22], ALU.mult, ALU.add)
                    if b >= 2:
                        dve.wait_ge(s_y, b - 1)
                    dve.tensor_tensor(hr[b % 2], aa[:, 0, :], aa[:, 1, :], ALU.subtract).then_inc(s_hr, 1)
                    dve.wait_ge(s_hr, b + 1)
                if 2 <= c <= NC + 1:
                    b = c - 2
                    dve.wait_ge(s_y, b + 1)
                    for h in range(2):
                        rows = xs[b % 4][:, 2 * h:2 * h + 2, :]
                        last = dve.tensor_tensor(rows, rows, bank[6 + h][:].rearrange("p (i d) -> p i d", d=D), ALU.add)
                    last.then_inc(s_x2, 1)
                    dve.wait_ge(s_x2, b + 1)
                    if b >= 2:
                        dve.wait_ge(s_nb3, b - 1)
                    row_stats(xs[b % 4], 2 + b % 2, nmean[:, b * CT:(b + 1) * CT], s_st3)
                if c >= 3:
                    b = c - 3
                    dve.wait_ge(s_lg, b + 1)
                    dve.tensor_copy(logits[:, b * CT:(b + 1) * CT, :],
                                    bank[5][:, 0:CT * E].rearrange("p (i e) -> p i e", e=E)).then_inc(s_lgsb, 1)
            dve.wait_ge(s_lgsb, NC)
            route(2)
            ffn(2)

        @block.tensor
        def _(pe):
            pe.wait_ge(const_done, 1)
            pe.wait_ge(par_in, 16 * NPAR)
            for c in range(DC):
                pe.transpose(bank[4][:, c * N:(c + 1) * N], braw[:, c * P:(c + 1) * P], ident[:])
                pe.transpose(bank[4][:, DC * N + c * P:DC * N + (c + 1) * P], craw[:, c, :], ident[:])
            pe.transpose(bank[5][:, 0:E * FC], b1raw, ident[0:E * FC, 0:E * FC]).then_inc(par_t, 1)

            def turn_rows(src, banks, done):
                for d in range(DC):
                    for i in range(CT):
                        last = pe.transpose(banks[d][:, i * P:(i + 1) * P], src[:, i, d * P:(d + 1) * P], ident[:])
                last.then_inc(done, 1)

            def route_logits(src, dst, done):
                for i in range(CT):
                    for d in range(DC):
                        last = pe.matmul(dst[:, i * E:(i + 1) * E], src[:, d, i * P:(i + 1) * P], wr[:, d, :],
                                         start=(d == 0), stop=(d == DC - 1))
                last.then_inc(done, 1)

            def entry(turn, k):
                c = chunk(turn, k)[0]
                pe.wait_ge(a_xn, c + 1)
                if has(c, 2):
                    pe.wait_ge(a_xt, c - 1)
                turn_rows(xnc[k], bank[2 * k:2 * k + 2], a_t)
                pe.wait_ge(a_xt, c + 1)
                if has(c, 2):
                    pe.wait_ge(a_lgsb, c - 1)
                route_logits(xtc, bank[6 + k][:, 0:CT * E], a_lg)
            Chain(pe, None).over_chunks(entry)

            def route(ph):
                s = S[ph]
                onehot = rt[3][:, 0:E * NJ // 2].bitcast(BF16)
                pe.wait_ge(s["onehot"], 1)
                pe.matmul(bank[5][:, 0:256], earlier[:], onehot, start=True, stop=True)
                pe.matmul(bank[5][:, 256:512], ones[:], onehot, start=True, stop=True).then_inc(s["counts"], 1)
                pe.wait_ge(s["pos"], 1)
                for g in range(NJ // GR):
                    pe.wait_ge(s["row"], g + 1)
                    for i in range(GR):
                        j = GR * g + i
                        last = pe.matmul(bank[4][:, 0:4 * NT], onerow[g % 2][:, i, :],
                                         sval[:, j, :, :].rearrange("p a b -> p (a b)"),
                                         start=(j == 0), stop=(j == NJ - 1))
                    last.then_inc(s["rowused"], 1)
                pe.wait_ge(s["sorted_sb"], 1)

            def ffn(ph):
                s = S[ph]

                def turn_tile(turn, k):
                    q, k, turn = tile(turn, k)
                    pe.wait_ge(s["xn"], q + 1)
                    if has(q, 2):
                        pe.wait_ge(s["xt"], q - 1)
                    for d in range(DC):
                        last = pe.transpose(bank[6 + k % 2][:, d * P:(d + 1) * P], xng[k % 2][:, d * P:(d + 1) * P],
                                            ident[:])
                    last.then_inc(s["turned"], 1)

                def expert(q):
                    e = pe.value_load(eid[0:1, at(q, 1)], min_val=0, max_val=E - 1)
                    return pe.snap(e * (2 * WB))

                def product1(turn, k, w):
                    q, k, turn = tile(turn, k)
                    pe.wait_ge(s["xt"], q + 1)
                    for half in range(2):
                        acc = bank[2 * (k % 2) + half]
                        if has(q, 2):
                            pe.wait_ge(s["gelu"], q * 2 - 3 + half)
                        for f in range(4 * half, 4 * half + 4):
                            weights = [big[:, bass.ds(w + 2 * (wpart * WE + d * F + f * P), 2 * P)].bitcast(F16)
                                       for wpart in range(2) for d in range(DC)]
                            for block_of in weights:
                                pe.lower_ap(block_of, for_matmul_weights=True)
                            n = 0
                            for wpart in range(2):
                                for d in range(DC):
                                    for xpart in range(2 - wpart):
                                        last = pe.matmul(acc[:, (f % 4) * P:(f % 4 + 1) * P], weights[wpart * DC + d],
                                                         xts[k % 2][:, xpart, d, :], start=(n == 0), stop=(n == 5))
                                        n += 1
                        last.then_inc(s["m1"], 1)

                def product2(turn, k, w):
                    q, k, turn = tile(turn, k)
                    acc = bank[4 + k % 2]
                    if has(q, 2):
                        pe.wait_ge(s["o"], q - 1)
                    for f in range(FC):
                        if f % 4 == 0:
                            pe.wait_ge(s["hsplit"], q * 2 + f // 4 + 1)
                            both = [big[:, bass.ds(w + (WB + g * 4 * D), 4 * D)].bitcast(F16) for g in range(f, f + 4)]
                            for block_of in both:
                                pe.lower_ap(block_of)
                        rhs = both[f % 4]
                        pe.matmul(acc[:], hs[k % 2][:, 0, f, :], rhs, start=(f == 0), stop=False)
                        last = pe.matmul(acc[:, 0:D], hs[k % 2][:, 1, f, :], rhs[:, 0:D], start=False, stop=(f == FC - 1))
                    last.then_inc(s["m2"], 1)

                def step(turn, k):
                    q = tile(turn, k)[0]
                    w = expert(q)
                    if not isinstance(q, int) or q + 1 < NT:
                        w_next = expert(q + 1)
                    if not isinstance(q, int) or q + 2 < NT:
                        turn_tile(turn, k + 2)
                    if not isinstance(q, int) or q + 1 < NT:
                        product1(turn, k + 1, w_next)
                    product2(turn, k, w)

                turn_tile(0, 0)
                turn_tile(0, 1)
                product1(0, 0, expert(0))
                over_tiles(pe, step)

            route(1)
            ffn(1)
            for c in range(NC + 2):
                if c < NC:
                    pe.wait_ge(s_un, c + 1)
                    if c >= 1:
                        pe.wait_ge(s_uts, c)
                    turn_rows(uns[c % 2], bank[0:2], s_ut)
                    pe.wait_ge(s_uts, c + 1)
                    if c >= 1:
                        pe.wait_ge(s_in, c)
                    for d in range(DC):
                        last = pe.matmul(bank[4][:], bt[:, d, :], uts[:, d, :], start=(d == 0), stop=(d == DC - 1))
                    last.then_inc(s_g, 1)
                if 1 <= c <= NC:
                    b = c - 1
                    pe.wait_ge(s_hr, b + 1)
                    if b >= 1:
                        pe.wait_ge(s_x2, b)
                    for i in range(CT):
                        last = pe.matmul(bank[6 + i // 2][:, (i % 2) * D:(i % 2 + 1) * D],
                                         hr[b % 2][:, i * P:(i + 1) * P], ct[:], start=True, stop=True)
                    last.then_inc(s_y, 1)
                if c >= 2:
                    b = c - 2
                    pe.wait_ge(s_xn3, b + 1)
                    if b >= 1:
                        pe.wait_ge(s_xt3, b)
                    turn_rows(xn3[b % 2], bank[2:4], s_t3)
                    pe.wait_ge(s_xt3, b + 1)
                    if b >= 1:
                        pe.wait_ge(s_lgsb, b)
                    route_logits(xt3, bank[5][:, 0:CT * E], s_lg)
            route(2)
            ffn(2)


INPUTS = ("L0_attn_u L0_attn_A_real L0_attn_A_imag L0_attn_B L0_attn_C L0_ffn_Wr L0_ffn_W1 L0_ffn_b1 L0_ffn_W2 "
          "L0_ffn_b2").split()


def kernel(**inputs):
    import concourse.bacc as bacc
    import numpy as np
    from concourse.bass_utils import run_bass_kernel_spmd

    nc = bacc.Bacc("TRN2", target_bir_lowering=False, num_devices=1)
    arrays = {name: np.ascontiguousarray(inputs[name]) for name in INPUTS}
    aps = {name: nc.dram_tensor(name, a.shape, F32, kind="ExternalInput").ap() for name, a in arrays.items()}
    aps["out"] = nc.dram_tensor("out", (1, T, D), F32, kind="ExternalOutput").ap()
    macaron(nc, aps)
    return run_bass_kernel_spmd(nc, [arrays], core_ids=[0]).results[0]["out"]
```

```python
from contextlib import ExitStack

import concourse.bass as bass
from concourse import mybir

F32 = mybir.dt.float32
F16 = mybir.dt.float16
BF16 = mybir.dt.bfloat16
I32 = mybir.dt.int32
U32 = mybir.dt.uint32
U8 = mybir.dt.uint8
ALU = mybir.AluOpType
ACT = mybir.ActivationFunctionType
AX = mybir.AxisListType.X
ABSMAX = bass.bass_isa.ReduceOp.absmax

P = 128
T = 4096
D = 256
DC = D // P
E = 8
F = 1024
FC = F // P
N = 128
NJ = T // P
CH = 512
CT = CH // P
NC = T // CH
NT = NJ + E - 1
LATE = 4
XS = 5
GR = 8
RING = 6
EPS = 1e-5
DT = 0.01
BIG = 8192.0
SX = 2.0 ** 10
TOP = 2.0 ** 14
HB = float(D)
EXPONENT = 0x7F800000
TINY = 1e-30
WE = DC * F
WB = 2 * WE * 2
LAG = 4
TURNS = NT // RING
AHEAD = 2


def hold(engine, held, sem, value):
    engine.wait_ge(sem, value)
    if not isinstance(value, int):
        engine.sem_inc(held, 1)


def tile(turn, k):
    turn, k = turn + k // RING, k % RING
    return turn * RING + k, k, turn


def over_tiles(engine, step):
    for k in range(RING):
        step(0, k)
    with engine.Fori(1, TURNS) as it:
        for k in range(RING):
            step(it, k)
    for k in range(NT - TURNS * RING):
        step(TURNS, k)


def chunk(turn, k):
    turn, k = turn + k // 2, k % 2
    return turn * 2 + k, k, turn


def before(q, end):
    return not isinstance(q, int) or q < end


def has(q, n):
    return not isinstance(q, int) or q >= n


class Chain:

    def __init__(self, engine, sem, held=None):
        self.engine, self.sem, self.held = engine, sem, held
        self.n = 0
        self.turns = 0

    def link(self, instruction):
        instruction.then_inc(self.sem, 1)
        self.n += 1
        hold(self.engine, self.held, self.sem, self.turns + self.n)

    def over_chunks(self, step):
        start = self.n
        step(0, 0)
        step(0, 1)
        first = self.n - start
        with self.engine.Fori(1, NC // 2 - 1) as it:
            self.turns, self.n = it * first, start
            step(it, 0)
            step(it, 1)
            assert self.n - start == first
        self.turns, self.n = 0, start + first * (NC // 2 - 1)
        step(NC // 2 - 1, 0)
        step(NC // 2 - 1, 1)


def macaron(nc, A):
    u, out = A["L0_attn_u"][0], A["out"][0]
    x1_dram = nc.dram_tensor("x_after_ffn1", [T, D], F32, kind="Internal").ap()
    rec_dram = {ph: nc.dram_tensor(f"records_{ph}", [T, 4], F32, kind="Internal").ap() for ph in (1, 2)}
    x2_dram = nc.dram_tensor("x_after_ssm", [T, D], F32, kind="Internal").ap()
    ctx = ExitStack()
    with ctx:
        def sb(name, shape, dt=F32):
            return ctx.enter_context(nc.sbuf_tensor(name, shape, dt))

        def sem(name):
            return ctx.enter_context(nc.semaphore(name))

        ARENA = 15872
        big = sb("weights_arena", [P, 2 * E * WB + 4 * ARENA], U8)
        iota_r = sb("iota_r", [P, P])
        part = sb("part", [P, 1])
        part_i = sb("part_i", [P, 1], I32)
        iota_i = sb("iota_i", [P, P], I32)
        ident = sb("ident", [P, P])
        earlier = sb("earlier", [P, P], BF16)
        ones = sb("ones", [P, P], BF16)
        one = sb("one", [P, 1])
        rev = sb("rev", [P, E])
        iota_b = sb("iota_b", [P, P], BF16)
        tile_start = sb("tile_start", [P, NJ], BF16)
        mhalf = sb("mhalf", [P, CT])
        wr = sb("wr", [P, DC, E])
        bt = sb("bt", [P, DC, N])
        ct = sb("ct", [P, D])
        b1t = sb("b1t", [P, E * FC])
        ev = sb("ev", [P, 24])
        turn = sb("turn", [P, 2, CH])
        back = sb("back", [P, 2, CH])
        rho = sb("rho", [P, 1])
        state = sb("state", [P, 2])
        wmax2 = sb("wmax2", [P, 2, 2])
        wall2 = sb("wall2", [P, 2, 2])
        b1max = sb("b1max", [P, E])
        b1all = sb("b1all", [P, E])
        wall = sb("wall", [P, 2 * E])
        wpow = sb("wpow", [P, 2 * E])
        wscale = sb("wscale", [P, 2 * E])
        hpow = sb("hpow", [P, E])
        hscale = sb("hscale", [P, E])
        inv1 = sb("inv1", [P, E])
        inv2 = sb("inv2", [P, E])
        logits = sb("logits", [P, NJ, E])
        records = sb("records", [P, NJ, 4])
        nmean, rstd, halfp = (records[:, :, k] for k in range(3))
        sorti = sb("sorti", [P, NT, 3], I32)
        eid = sb("eid", [P, NT], I32)

        def view(at, *shape, dt=F32):
            size = 1
            for s in shape:
                size *= s
            words = size // 2 if dt in (F16, BF16) else size
            assert at + words <= ARENA
            a = big[:, 2 * E * WB + 4 * at:2 * E * WB + 4 * (at + words)].bitcast(dt)
            names = "abcd"[:len(shape)]
            if len(shape) == 1:
                return a
            return a.rearrange("p (" + " ".join(names) + ") -> p " + " ".join(names),
                               **{n: s for n, s in zip(names, shape)})

        xc = [view(8192 + k * CT * D, CT, D) for k in range(2)]
        xnc = [view(10240 + k * CT * D, CT, D) for k in range(2)]
        xtc = view(12288, DC, CH)
        sval = view(8192, NJ, 2, NT, dt=BF16)
        q1 = view(9472, NJ, NT, dt=BF16)
        onerow = view(10240, NJ, P, dt=BF16)
        rt = [view(14336 + 256 * k, E * NJ) for k in range(6)]
        hb = [view(k * 1024, FC, P) for k in range(2)]
        hs = [view(2048 + k * 1024, 2, FC, P, dt=F16) for k in range(2)]
        xg = [view(4096 + k * D, D) for k in range(RING)]
        xng = [view(5632 + k * D, D) for k in range(2)]
        xts = [view(6144 + k * 256, 2, DC, P, dt=F16) for k in range(2)]
        og = [view(6656 + k * D, D) for k in range(2)]
        b2b = view(7168, E * D)
        xs = [view(k * CT * D, CT, D) for k in range(XS)]
        uns = [view(5120 + k * CT * D, CT, D) for k in range(2)]
        uts = view(7168, DC, CH)
        xn3 = [view(8192 + k * CT * D, CT, D) for k in range(2)]
        xt3 = view(10240, DC, CH)
        mod = view(11264, 2, CH)
        aa = view(12288, 2, CH)
        zz = view(13312, 2, CH)
        hr = [view(14336 + k * CH, CH) for k in range(2)]
        gs = view(15360, CH)

        spare = sb("spare", [P, 1])
        recf = sb("recf", [P, RING, 4])
        gidx = sb("gidx", [P, RING, 2], I32)
        sidx = sb("sidx", [P, RING], I32)
        stats = sb("stats", [P, 4, CT, 6])
        mv = sb("mv", [P, 4, CT, 2])
        ve = sb("ve", [P, 4, CT])
        nm = sb("nm", [P, 2, CT])
        rs = sb("rs", [P, 2, CT])
        nb = sb("nb", [P, 4, CT])

        bank = [ctx.enter_context(nc.psum_tensor(f"bank{k}", [P, 512], F32)) for k in range(8)]

        par_in = sem("par_in")
        xload = [sem(f"xload{k}") for k in range(2)]
        wload = [sem(f"wload{k}") for k in range(4)]
        iota_done = sem("iota_done")
        const_done = sem("const_done")
        par_t = sem("par_t")
        par_sb = sem("par_sb")
        dve_chain = sem("dve_chain")
        pool_chain = sem("pool_chain")
        pool_held, act_held, dve_held = sem("pool_held"), sem("act_held"), sem("dve_held")
        rho_in = sem("rho_in")
        rho_out = sem("rho_out")
        a_stats = sem("a_stats")
        a_nb = sem("a_nb")
        s_nb = sem("s_nb")
        s_zi = sem("s_zi")
        s_zr = sem("s_zr")
        s_aa = sem("s_aa")
        s_nb3 = sem("s_nb3")
        a_xn = sem("a_xn")
        a_t = sem("a_t")
        a_xt = sem("a_xt")
        a_lg = sem("a_lg")
        a_lgsb = sem("a_lgsb")
        w_max = sem("w_max")
        w_all = sem("w_all")
        w_sc = sem("w_sc")
        w_hi = sem("w_hi")
        w_ws = sem("w_ws")
        w_lo = sem("w_lo")
        w_lo_dve = sem("w_lo_dve")
        s_gs = sem("s_gs")
        s_mi = sem("s_mi")
        b1_max = sem("b1_max")
        b1_all = sem("b1_all")
        inv_done = sem("inv_done")
        S = {}
        for ph in (1, 2):
            S[ph] = {k: sem(f"{k}_{ph}") for k in (
                "diff exps onehot counts rec_ready rec_stored q1 starts pos row rowused sorted_sb b2in gidx sidx xn turned "
                "xt_hi xt m1 gelu h_hi hsplit m2 o_chain o").split()}
            S[ph]["gath"] = [sem(f"gath{k}_{ph}") for k in range(RING)]
            S[ph]["scat"] = [sem(f"scat{k}_{ph}") for k in range(RING)]
        sx = [sem(f"s_load{k}") for k in range(XS)]
        s_store = [sem(f"s_store{k}") for k in range(XS)]
        s_stats, s_un, s_ut, s_uts, s_g, s_in, s_hr, s_y, s_x2, s_st3, s_xn3, s_t3, s_xt3, s_lg, s_lgsb = (
            sem(n) for n in ("s_stats s_un s_ut s_uts s_g s_in s_hr s_y s_x2 s_st3 s_xn3 s_t3 s_xt3 s_lg "
                             "s_lgsb").split())

        W1 = A["L0_ffn_W1"].rearrange("e (c p) f -> e p c f", p=P)
        W2 = A["L0_ffn_W2"].rearrange("e (c p) d -> e p c d", p=P)
        u_chunks = u.rearrange("(n i p) d -> n p i d", p=P, i=CT)
        x1_chunks = x1_dram.rearrange("(n i p) d -> n p i d", p=P, i=CT)
        x2_chunks = x2_dram.rearrange("(n i p) d -> n p i d", p=P, i=CT)

        def in_slot(k):
            return len(range(k, NT, RING))

        def at(q, n):
            return bass.ds(q * n, n)

        def weight_parts(e, which):
            a = big[:, bass.ds(e * (2 * WB) + which * WB, WB)].bitcast(F16)
            if which == 0:
                a = a.rearrange("p (h w) -> p h w", h=2)
            else:
                a = a.rearrange("p (f h d) -> p h f d", f=FC, h=2)
            return a[:, 0], a[:, 1]

        def pool_splits(k, which):
            return {(0, 0): 0, (1, 0): 1, (1, 1): 2}.get((k, which))

        def raw(e, which):
            a = big[:, bass.ds(e * (2 * WB) + (which + LAG) * WB, WB)].bitcast(F32)
            return a if which == 0 else a.rearrange("p (f d) -> p f d", f=FC)

        braw = view(14336, D)
        craw = view(14592, DC, N)
        b1raw = view(14848, P)[0:E * FC]
        araw = sb("araw", [P, 2])
        NPAR = 6
        block = ctx.enter_context(nc.Block())

        @block.sync
        def _(sp):
            def load_x(turn, k):
                c, k, turn = chunk(turn, k)
                if has(c, 2):
                    sp.wait_ge(a_xn, c - 1)
                sp.dma_start(xc[k], u_chunks[bass.ds(c, 1)].squeeze(0)).then_inc(xload[k], 16)

            def load_weights(turn, k):
                e, k, turn = chunk(turn, k)
                if has(e, 2):
                    sp.wait_ge(w_max, 2 * e - 2)
                for which, W in enumerate((W1, W2)):
                    sp.dma_start(big[:, bass.ds(e * (2 * WB) + (which + LAG) * WB, WB)].bitcast(F32)
                                 .rearrange("p (c f) -> p c f", c=W.shape[2]),
                                 W[bass.ds(e, 1)].squeeze(0)).then_inc(wload[2 * k + which], 16)

            def entry(turn, k):
                c = chunk(turn, k)[0]
                if before(c, NC - 1):
                    load_weights(turn, k + 1)
                if before(c, NC - 2):
                    load_x(turn, k + 2)
            load_x(0, 0)
            sp.dma_start(araw[:, 0:1], A["L0_attn_A_real"].unsqueeze(1)).then_inc(par_in, 16)
            sp.dma_start(araw[:, 1:2], A["L0_attn_A_imag"].unsqueeze(1)).then_inc(par_in, 16)
            sp.dma_start(braw, A["L0_attn_B"]).then_inc(par_in, 16)
            sp.dma_start(craw, A["L0_attn_C"].rearrange("(c p) n -> p c n", p=P)).then_inc(par_in, 16)
            sp.dma_start(wr[:], A["L0_ffn_Wr"].rearrange("(c p) e -> p c e", p=P)).then_inc(par_in, 16)
            sp.dma_start(b1raw, A["L0_ffn_b1"].rearrange("e (c p) -> (e c) p", p=P)).then_inc(par_in, 16)
            load_x(0, 1)
            load_weights(0, 0)
            Chain(sp, None).over_chunks(entry)

            def load_b2(ph):
                sp.wait_ge(S[ph]["sorted_sb"], 1)
                if ph == 1:
                    sp.wait_ge(w_lo, 3 * E // 2)
                    sp.wait_ge(w_lo_dve, E // 2)
                sp.dma_start(b2b, A["L0_ffn_b2"].rearrange("e d -> (e d)").partition_broadcast(P)) \
                    .then_inc(S[ph]["b2in"], 16)
            def store_records(ph):
                sp.wait_ge(S[ph]["rec_ready"], 1)
                sp.dma_start(rec_dram[ph].rearrange("(p j) k -> p j k", p=P), records[:]).then_inc(S[ph]["rec_stored"], 16)
            store_records(1)
            load_b2(1)
            for k in range(RING):
                sp.wait_ge(S[1]["scat"][k], 16 * in_slot(k))
            for c in range(XS):
                sp.dma_start(xs[c], x1_chunks[c]).then_inc(sx[c], 16)
            for c in range(NC):
                sp.wait_ge(s_x2, c + 1)
                sp.dma_start(x2_chunks[c], xs[c % XS]).then_inc(s_store[c % XS], 16)
                new = c - 1 + XS
                if c >= 1 and new < NC:
                    sp.wait_ge(s_store[new % XS], 16 * (new // XS))
                    sp.wait_ge(s_xn3, c)
                    sp.dma_start(xs[new % XS], x1_chunks[new]).then_inc(sx[new % XS], 16)
            store_records(2)
            load_b2(2)
            for k in range(RING):
                sp.wait_ge(S[2]["scat"][k], 16 * in_slot(k))

        @block.gpsimd
        def _(pool):
            chain = Chain(pool, pool_chain, pool_held)
            pool.iota(iota_i[:], [[1, P]], base=0, channel_multiplier=0).then_inc(iota_done, 1)
            pool.iota(part_i[:], [[0, 1]], base=0, channel_multiplier=1).then_inc(iota_done, 1)
            pool.memset(mhalf[:], -0.5).then_inc(iota_done, 1)
            hold(pool, pool_held, iota_done, 3)

            def inv_std(slot, means, to, ready, n, done):
                hold(pool, pool_held, ready, n)
                chain.link(pool.tensor_tensor(to, ve[:, slot, :], mhalf[:], ALU.pow))
                pool.tensor_tensor(nb[:, slot, :], means, to, ALU.mult).then_inc(done, 1)

            def entry_std(turn, k):
                c, k, turn = chunk(turn, k)
                if has(c, 2):
                    hold(pool, pool_held, a_xn, c - 1)
                inv_std(k, nmean[:, at(c, CT)], rstd[:, at(c, CT)], a_stats, c + 1, a_nb)

            def low_parts(turn, k):
                e, k, turn = chunk(turn, k)
                for which in range(2):
                    n = pool_splits(k, which)
                    if n is None:
                        continue
                    hi, lo = weight_parts(e, which)
                    hold(pool, pool_held, w_ws, turn * 3 + n + 1)
                    pool.tensor_tensor(lo, raw(e, which), hi, ALU.subtract).then_inc(w_lo, 1)

            def entry(turn, k):
                c = chunk(turn, k)[0]
                if before(c, NC - 1):
                    entry_std(turn, k + 1)
                hold(pool, pool_held, w_max, 2 * c + 2)
                pool.partition_all_reduce(wall2[:, k, :], wmax2[:, k, :], P, ABSMAX).then_inc(w_all, 1)
                if has(c, 1):
                    low_parts(turn, k - 1)
            entry_std(0, 0)
            hold(pool, pool_held, rho_in, 1)
            pool.tensor_tensor(ev[:, 13:14], ev[:, 12:13], mhalf[:, 0:1], ALU.pow).then_inc(rho_out, 1)
            chain.over_chunks(entry)
            hold(pool, pool_held, b1_max, 1)
            pool.partition_all_reduce(b1all[:], b1max[:], P, ABSMAX).then_inc(b1_all, 1)
            low_parts(NC // 2 - 1, 1)

            def ffn(ph, src, dst):
                s = S[ph]
                hold(pool, pool_held, s["q1"], 1)
                pool.tensor_tensor(sval[:, :, 0, :], q1, tile_start[:].unsqueeze(2).to_broadcast([P, NJ, NT]), ALU.mult) \
                    .then_inc(s["starts"], 1)
                hold(pool, pool_held, s["sorted_sb"], 1)
                if ph == 2:
                    for k in range(XS):
                        hold(pool, pool_held, s_store[k], 16 * len(range(k, NC, XS)))
                else:
                    hold(pool, pool_held, w_lo, 3 * E // 2)
                    hold(pool, pool_held, w_lo_dve, E // 2)

                def fetch(turn, k):
                    q, k, turn = tile(turn, k)
                    if has(q, RING):
                        hold(pool, pool_held, s["o"], q - RING + 1)
                    pool.tensor_copy(gidx[:, k, :], sorti[:, at(q, 1), 0:2].squeeze(1)).then_inc(s["gidx"], 1)
                    hold(pool, pool_held, s["gidx"], q + 1)
                    for to, source, index in ((xg[k], src, 0), (recf[:, k, :], rec_dram[ph], 1)):
                        if index == 1 and isinstance(q, int) and q == 0:
                            hold(pool, pool_held, s["rec_stored"], 16)
                        pool.indirect_dma_start(to, None, source, bass.IndirectOffsetOnAxis(
                            ap=gidx[:, k, index:index + 1].bitcast(U32), axis=0)).then_inc(s["gath"][k], 16)

                def norm(turn, k):
                    q, k, turn = tile(turn, k)
                    if has(q, 2):
                        hold(pool, pool_held, s["turned"], q - 1)
                    hold(pool, pool_held, s["gath"][k], turn * 32 + 32)
                    pool.tensor_scalar(xng[k % 2], xg[k], recf[:, k, 0:1], recf[:, k, 1:2], ALU.add, ALU.mult) \
                        .then_inc(s["xn"], 1)

                def scatter(turn, k):
                    q, k, turn = tile(turn, k)
                    hold(pool, pool_held, s["o"], q + 1)
                    pool.tensor_copy(sidx[:, k:k + 1], sorti[:, at(q, 1), 2:3].squeeze(1)).then_inc(s["sidx"], 1)
                    hold(pool, pool_held, s["sidx"], q + 1)
                    pool.indirect_dma_start(dst, bass.IndirectOffsetOnAxis(ap=sidx[:, k:k + 1].bitcast(U32), axis=0),
                                            og[k % 2], None, bounds_check=T - 1, oob_is_err=False) \
                        .then_inc(s["scat"][k], 16)

                def step(turn, k):
                    q = tile(turn, k)[0]
                    if has(q, AHEAD):
                        norm(turn, k - AHEAD)
                    if has(q, RING):
                        scatter(turn, k - RING)
                    fetch(turn, k)

                over_tiles(pool, step)
                left = NT - TURNS * RING
                for k in range(left - AHEAD, left):
                    norm(TURNS, k)
                for k in range(left - RING, left):
                    scatter(TURNS, k)

            ffn(1, u, x1_dram)
            for c in range(-2, NC + 1):
                if 0 <= c < NC:
                    hold(pool, pool_held, s_zr, c + 1)
                    pool.tensor_tensor(aa[:, 0, :], zz[:, 0, :], back[:, 0, :], ALU.mult)
                    hold(pool, pool_held, s_zi, c + 1)
                    pool.tensor_tensor(aa[:, 1, :], zz[:, 1, :], back[:, 1, :], ALU.mult).then_inc(s_aa, 1)
                    hold(pool, pool_held, s_aa, c + 1)
                    if c >= 2:
                        hold(pool, pool_held, s_y, c - 1)
                    pool.tensor_tensor(hr[c % 2], aa[:, 0, :], aa[:, 1, :], ALU.add).then_inc(s_hr, 1)
                if c + 2 < NC:
                    n = c + 2
                    if n >= 2:
                        hold(pool, pool_held, s_un, n - 1)
                    inv_std(n % 2, nm[:, n % 2, :], rs[:, n % 2, :], s_stats, n + 1, s_nb)
                if 0 <= c + 1 < NC:
                    hold(pool, pool_held, s_gs, c + 2)
                    if c >= 0:
                        hold(pool, pool_held, s_zi, c + 1)
                    pool.tensor_tensor(mod[:, 1, :], gs, turn[:, 1, :], ALU.mult).then_inc(s_mi, 1)
                if c >= 1:
                    d = c - 1
                    if d >= 2:
                        hold(pool, pool_held, s_xn3, d - 1)
                    inv_std(2 + d % 2, nmean[:, d * CT:(d + 1) * CT], rstd[:, d * CT:(d + 1) * CT], s_st3, d + 1, s_nb3)
            ffn(2, x2_dram, out)

        @block.scalar
        def _(act):
            def normalise(slot, src, dst, scales, ready, n, done):
                hold(act, act_held, ready, n)
                for i in range(CT):
                    last = act.activation(dst[:, i, :], src[:, i, :], ACT.Identity, bias=nb[:, slot, i:i + 1],
                                          scale=scales(i))
                last.then_inc(done, 1)

            def entry_rows(turn, k):
                c, k, turn = chunk(turn, k)
                if has(c, 2):
                    hold(act, act_held, a_t, c - 1)
                normalise(k, xc[k], xnc[k], lambda i: rstd[:, bass.ds(c * CT + i, 1)], a_nb, c + 1, a_xn)

            def entry(turn, k):
                c = chunk(turn, k)[0]
                if before(c, NC - 1):
                    entry_rows(turn, k + 1)
                hold(act, act_held, a_t, c + 1)
                if has(c, 1):
                    hold(act, act_held, a_lg, c)
                for d in range(DC):
                    last = act.copy(xtc[:, d, :], bank[2 * k + d][:])
                last.then_inc(a_xt, 1)
                hold(act, act_held, w_sc, c + 1)
                for which in range(2):
                    hi, lo = weight_parts(c, which)
                    src = raw(c, which)
                    scale = wscale[:, bass.ds(c * 2 + which, 1)]
                    n = pool_splits(k, which)
                    if has(c, 2):
                        if n is None:
                            hold(act, act_held, w_lo_dve, turn)
                        else:
                            hold(act, act_held, w_lo, turn * 3 + n - 2)
                    act.activation(hi, src, ACT.Copy, scale=scale).then_inc(w_hi, 1)
                    if n is not None:
                        act.activation(src, src, ACT.Copy, scale=scale).then_inc(w_ws, 1)
            entry_rows(0, 0)
            Chain(act, None).over_chunks(entry)

            def ffn(ph):
                s = S[ph]
                act.wait_ge(s["diff"], 1)
                act.activation(rt[1], rt[0], ACT.Exp).then_inc(s["exps"], 1)
                act.activation(spare[:], mhalf[:, 0:1], ACT.Gelu)
                act.wait_ge(s["sorted_sb"], 1)
                act.wait_ge(inv_done, 1)

                def step(turn, k):
                    q, k, turn = tile(turn, k)
                    e = act.value_load(eid[0:1, at(q, 1)], min_val=0, max_val=E - 1)
                    for half in range(2):
                        act.wait_ge(s["m1"], q * 2 + half + 1)
                        if half == 0 and (not isinstance(q, int) or q >= 2):
                            act.wait_ge(s["hsplit"], q * 2 - 2)
                        for f in range(half * 4, half * 4 + 4):
                            src = bank[2 * (k % 2) + half][:, (f % 4) * P:(f % 4 + 1) * P]
                            last = act.activation(hb[k % 2][:, f, :], src, ACT.Gelu,
                                                  bias=b1t[:, bass.ds(e * FC + f, 1)], scale=inv1[:, bass.ds(e, 1)])
                        last.then_inc(s["gelu"], 1)

                over_tiles(act, step)
            ffn(1)
            act.activation(spare[:], mhalf[:, 0:1], ACT.Exp)
            for c in range(-2, NC + 2):
                if 0 <= c + 1 < NC:
                    act.wait_ge(s_ut, c + 2)
                    if c >= 0:
                        act.wait_ge(s_g, c + 1)
                    for d in range(DC):
                        last = act.copy(uts[:, d, :], bank[d][:])
                    last.then_inc(s_uts, 1)
                if c >= 2:
                    d3 = c - 2
                    if d3 >= 2:
                        act.wait_ge(s_t3, d3 - 1)
                    normalise(2 + d3 % 2, xs[d3 % XS], xn3[d3 % 2], lambda i: rstd[:, d3 * CT + i:d3 * CT + i + 1],
                              s_nb3, d3 + 1, s_xn3)
                if 0 <= c + 1 < NC:
                    act.wait_ge(s_g, c + 2)
                    if c >= 0:
                        act.wait_ge(s_mi, c + 1)
                        act.wait_ge(s_in, c + 1)
                    act.copy(gs, bank[4][:]).then_inc(s_gs, 1)
                if c >= 2:
                    act.wait_ge(s_t3, d3 + 1)
                    if d3 >= 1:
                        act.wait_ge(s_lg, d3)
                    for d in range(DC):
                        last = act.copy(xt3[:, d, :], bank[2 + d][:])
                    last.then_inc(s_xt3, 1)
                for n in {-2: (0, 1), -1: ()}.get(c, (c + 2,) if c + 2 < NC else ()):
                    if n >= 2:
                        act.wait_ge(s_ut, n - 1)
                    normalise(n % 2, xs[n % XS], uns[n % 2], lambda i: rs[:, n % 2, i:i + 1], s_nb, n + 1, s_un)
            ffn(2)

        @block.vector
        def _(dve):
            chain = Chain(dve, dve_chain, dve_held)
            link = chain.link
            dve.wait_ge(iota_done, 2)
            dve.tensor_copy(iota_r[:], iota_i[:])
            link(dve.tensor_copy(part[:], part_i[:]))
            dve.tensor_scalar(ident[:], iota_r[:], part[:], None, ALU.is_equal).then_inc(const_done, 1)
            dve.tensor_scalar(earlier[:], iota_r[:], part[:], None, ALU.is_gt)
            dve.memset(ones[:], 1.0)
            dve.memset(one[:], 1.0)
            dve.tensor_scalar(rev[:], iota_r[:, 0:E], -1.0, float(E), ALU.mult, ALU.add)
            dve.tensor_scalar(tile_start[:], iota_r[:, 0:NJ], float(P), -BIG, ALU.mult, ALU.add)
            dve.tensor_copy(iota_b[:], iota_r[:])
            dve.memset(records[:, :, 3], 0.0)

            def row_stats(src, k, means, done):
                for i in range(CT):
                    last = dve.bn_stats(stats[:, k, i, :], src[:, i, :])
                link(last)
                for i in range(CT):
                    last = dve.bn_aggr(mv[:, k, i, :], stats[:, k, i, :])
                link(last)
                dve.tensor_scalar(means, mv[:, k, :, 0], -1.0, None, ALU.mult)
                dve.tensor_scalar(ve[:, k, :], mv[:, k, :, 1], EPS, None, ALU.add).then_inc(done, 1)

            def entry_stats(turn, k):
                c, k, turn = chunk(turn, k)
                dve.wait_ge(xload[k], turn * 16 + 16)
                if has(c, 2):
                    dve.wait_ge(a_nb, c - 1)
                row_stats(xc[k], k, nmean[:, at(c, CT)], a_stats)

            def entry_logits(turn, k):
                c, k, turn = chunk(turn, k)
                dve.wait_ge(a_lg, c + 1)
                dve.tensor_copy(logits[:, at(c, CT), :],
                                bank[6 + k][:, 0:CT * E].rearrange("p (i e) -> p i e", e=E)).then_inc(a_lgsb, 1)

            def entry(turn, k):
                c = chunk(turn, k)[0]
                if before(c, NC - 1):
                    entry_stats(turn, k + 1)
                for which in range(2):
                    dve.wait_ge(wload[2 * k + which], turn * 16 + 16)
                    dve.tensor_reduce(wmax2[:, k, which:which + 1],
                                      big[:, bass.ds(c * (2 * WB) + (which + LAG) * WB, WB)].bitcast(F32),
                                      AX, ALU.max, apply_absolute_value=True).then_inc(w_max, 1)
                if has(c, 1):
                    entry_logits(turn, k - 1)
                if k == 1:
                    hi, lo = weight_parts(c - 1, 1)
                    dve.wait_ge(w_hi, 2 * c)
                    dve.scalar_tensor_tensor(lo, raw(c - 1, 1), wscale[:, bass.ds(c * 2 - 1, 1)], hi,
                                             ALU.mult, ALU.subtract).then_inc(w_lo_dve, 1)
                two = at(c, 2)
                dve.wait_ge(w_all, c + 1)
                link(dve.tensor_scalar(wall[:, two], wall2[:, k, :], TINY, None, ALU.max))
                link(dve.tensor_scalar(wpow[:, two].bitcast(I32), wall[:, two].bitcast(I32), EXPONENT, None,
                                       ALU.bitwise_and))
                link(dve.reciprocal(wscale[:, two], wpow[:, two]))
                dve.tensor_scalar(wscale[:, two], wscale[:, two], TOP, None, ALU.mult).then_inc(w_sc, 1)
            entry_stats(0, 0)
            dve.wait_ge(par_t, 1)
            dve.tensor_copy(bt[:], bank[4][:, 0:DC * N].rearrange("p (c n) -> p c n", c=DC))
            dve.tensor_copy(ct[:], bank[4][:, DC * N:DC * N + D]).then_inc(par_sb, 1)
            link(dve.tensor_copy(b1t[:], bank[5][:, 0:E * FC]))
            dve.tensor_reduce(b1max[:], b1t[:].rearrange("p (e c) -> p e c", c=FC), AX, ALU.max,
                              apply_absolute_value=True).then_inc(b1_max, 1)
            col = lambda k: ev[:, k:k + 1]
            link(dve.tensor_scalar(ev[:, 0:2], araw[:], DT / 2, None, ALU.mult))
            dve.tensor_scalar(col(2), col(0), -1.0, 1.0, ALU.mult, ALU.add)
            dve.tensor_scalar(col(3), col(0), 1.0, None, ALU.add)
            link(dve.tensor_tensor(col(4), col(1), col(1), ALU.mult))
            dve.scalar_tensor_tensor(col(5), col(2), col(2), col(4), ALU.mult, ALU.add)
            link(dve.scalar_tensor_tensor(col(6), col(3), col(2), col(4), ALU.mult, ALU.subtract))
            dve.reciprocal(col(7), col(5))
            link(dve.tensor_tensor(col(8), col(2), col(3), ALU.add))
            link(dve.tensor_tensor(col(9), col(8), col(1), ALU.mult))
            dve.tensor_tensor(col(10), col(6), col(7), ALU.mult)
            link(dve.tensor_tensor(col(11), col(9), col(7), ALU.mult))
            dve.tensor_scalar(col(14), col(2), col(7), DT ** 0.5, ALU.mult, ALU.mult)
            dve.tensor_scalar(col(15), col(1), col(7), DT ** 0.5, ALU.mult, ALU.mult)
            link(dve.tensor_tensor(col(16), col(10), col(10), ALU.mult))
            dve.scalar_tensor_tensor(col(12), col(11), col(11), col(16), ALU.mult, ALU.add).then_inc(rho_in, 1)
            dve.wait_ge(rho_in, 1)
            dve.wait_ge(rho_out, 1)
            dve.tensor_tensor(rho[:], col(12), col(13), ALU.mult)
            dve.tensor_scalar(turn[:, 0, 0:1], col(10), col(13), None, ALU.mult)
            link(dve.tensor_scalar(turn[:, 1, 0:1], col(11), col(13), None, ALU.mult))
            chain.over_chunks(entry)
            entry_logits(NC // 2 - 1, 1)
            dve.wait_ge(a_lgsb, NC)

            def double(n):
                c0, s0 = turn[:, 0, 0:n], turn[:, 1, 0:n]
                cn, sn = turn[:, 0, n - 1:n], turn[:, 1, n - 1:n]
                dve.tensor_scalar(back[:, 0, 0:n], s0, sn, None, ALU.mult)
                link(dve.tensor_scalar(back[:, 1, 0:n], c0, sn, None, ALU.mult))
                dve.scalar_tensor_tensor(turn[:, 0, n:2 * n], c0, cn, back[:, 0, 0:n], ALU.mult, ALU.subtract)
                link(dve.scalar_tensor_tensor(turn[:, 1, n:2 * n], s0, cn, back[:, 1, 0:n], ALU.mult, ALU.add))

            def readout(part):
                col_a, col_b, how = (0, 1, ALU.subtract) if part == 0 else (1, 0, ALU.add)
                tmp = aa[:, part, :]
                link(dve.tensor_scalar(tmp, turn[:, col_b, :], col(15), None, ALU.mult))
                link(dve.scalar_tensor_tensor(back[:, part, :], turn[:, col_a, :], col(14), tmp, ALU.mult, how))

            def product_scales():
                dve.wait_ge(b1_all, 1)
                w2x = lambda t, k: t[:, 0:2 * E].rearrange("p (e k) -> p k e", k=2)[:, k, :]
                link(dve.scalar_tensor_tensor(hpow[:], w2x(wall, 0), HB, b1all[:], ALU.mult, ALU.add))
                link(dve.tensor_scalar(hpow[:].bitcast(I32), hpow[:].bitcast(I32), EXPONENT, None, ALU.bitwise_and))
                link(dve.reciprocal(hscale[:], hpow[:]))
                dve.tensor_scalar(hscale[:], hscale[:], TOP, None, ALU.mult)
                dve.tensor_scalar(inv1[:], w2x(wpow, 0), 1.0 / (TOP * SX), None, ALU.mult)
                link(dve.tensor_scalar(hpow[:], hpow[:], 1.0 / TOP, None, ALU.mult))
                dve.scalar_tensor_tensor(inv2[:], w2x(wpow, 1), 1.0 / TOP, hpow[:], ALU.mult, ALU.mult) \
                    .then_inc(inv_done, 1)

            def route(ph):
                s = S[ph]
                je = lambda a: a.rearrange("p (j e) -> p j e", e=E)
                ej = lambda a: a.rearrange("p (e j) -> p e j", e=E)
                swap = lambda a: a.rearrange("p (e j) -> p j e", e=E)
                over_e = lambda a: a.unsqueeze(2).to_broadcast([P, NJ, E])
                top = rt[5][:, 0:NJ]
                first = rt[5][:, NJ:2 * NJ]
                pos = rt[5][:, 2 * NJ:3 * NJ]
                whole = rt[5][:, 3 * NJ:4 * NJ]
                small = lambda k: rt[5][:, 5 * NJ + 8 * k:5 * NJ + 8 * k + 8]
                link(dve.tensor_reduce(top, logits[:], AX, ALU.max))
                link(dve.tensor_tensor(je(rt[2]), logits[:], over_e(top), ALU.is_equal))
                link(dve.tensor_tensor(je(rt[2]), je(rt[2]), rev[:].unsqueeze(1).to_broadcast([P, NJ, E]), ALU.mult))
                link(dve.tensor_reduce(first, je(rt[2]), AX, ALU.max))
                onehot = rt[3][:, 0:E * NJ // 2].bitcast(BF16)
                dve.tensor_tensor(swap(onehot), rev[:].unsqueeze(1).to_broadcast([P, NJ, E]), over_e(first),
                                  ALU.is_equal).then_inc(s["onehot"], 1)
                dve.tensor_tensor(je(rt[0]), logits[:], over_e(top), ALU.subtract).then_inc(s["diff"], 1)
                if ph == 1:
                    product_scales()
                dve.wait_ge(s["counts"], 1)
                link(dve.tensor_tensor_scan(rt[4], one[:].to_broadcast([P, E * NJ]), bank[5][:, 256:512], 0.0,
                                            ALU.mult, ALU.add))
                dve.tensor_tensor(rt[2], rt[4], bank[5][:, 256:512], ALU.subtract)
                ends = ej(rt[4])[:, :, NJ - 1]
                cnt, tiles, tend, shift = small(0), small(1), small(2), small(3)
                dve.tensor_tensor(cnt[:, 1:E], ends[:, 1:E], ends[:, 0:E - 1], ALU.subtract)
                link(dve.tensor_copy(cnt[:, 0:1], ends[:, 0:1]))
                link(dve.tensor_scalar(tiles.bitcast(I32), cnt, float(P - 1), None, ALU.add))
                link(dve.tensor_scalar(tend.bitcast(I32), tiles.bitcast(I32), 7, None, ALU.arith_shift_right))
                link(dve.tensor_copy(tiles, tend.bitcast(I32)))
                link(dve.tensor_tensor_scan(tend, one[:].to_broadcast([P, E]), tiles, 0.0, ALU.mult, ALU.add))
                link(dve.tensor_tensor(tiles, tend, tiles, ALU.subtract))
                link(dve.tensor_tensor(cnt, ends, cnt, ALU.subtract))
                link(dve.scalar_tensor_tensor(shift, tiles, float(P), cnt, ALU.mult, ALU.subtract))
                link(dve.tensor_tensor(rt[2], rt[2], bank[5][:, 0:256], ALU.add))
                link(dve.tensor_tensor(ej(rt[2]), ej(rt[2]), shift.unsqueeze(2).to_broadcast([P, E, NJ]), ALU.add))
                link(dve.tensor_tensor(rt[2], rt[2], onehot, ALU.mult))
                link(dve.tensor_reduce(pos, swap(rt[2]), AX, ALU.add))
                posi = whole.bitcast(I32)
                link(dve.tensor_copy(posi, pos))
                sloti = pos.bitcast(I32)
                link(dve.tensor_scalar(sloti, posi, P - 1, None, ALU.bitwise_and))
                tli = first.bitcast(I32)
                link(dve.tensor_scalar(tli, posi, 7, None, ALU.arith_shift_right))
                slot_b, tile_b = rt[5][:, 192:208].bitcast(BF16), rt[5][:, 208:224].bitcast(BF16)
                dve.tensor_copy(slot_b, sloti)
                link(dve.tensor_copy(tile_b, tli))
                dve.tensor_tensor(q1, iota_b[:, 0:NT].unsqueeze(1).to_broadcast([P, NJ, NT]),
                                  tile_b.unsqueeze(2).to_broadcast([P, NJ, NT]), ALU.is_equal).then_inc(s["q1"], 1)
                dve.wait_ge(s["q1"], 1)
                dve.tensor_scalar(sval[:, :, 1, :], q1, part[:], None, ALU.mult).then_inc(s["pos"], 1)
                for g in range(NJ // GR):
                    rows = slice(GR * g, GR * g + GR)
                    dve.tensor_tensor(onerow[:, rows, :], iota_b[:].unsqueeze(1).to_broadcast([P, GR, P]),
                                      slot_b[:, rows].unsqueeze(2).to_broadcast([P, GR, P]),
                                      ALU.is_equal).then_inc(s["row"], 1)
                ntc = view(12288, NT, E)
                link(dve.tensor_tensor(ntc, iota_r[:, 0:NT].unsqueeze(2).to_broadcast([P, NT, E]),
                                       tend.unsqueeze(1).to_broadcast([P, NT, E]), ALU.is_ge))
                eidf = view(12800, NT)
                link(dve.tensor_reduce(eidf, ntc, AX, ALU.add))
                dve.tensor_scalar(eid[:], eidf, float(E - 1), None, ALU.min)
                dve.wait_ge(s["exps"], 1)
                link(dve.tensor_reduce(halfp, je(rt[1]), AX, ALU.add))
                link(dve.reciprocal(halfp, halfp))
                dve.tensor_scalar(halfp, halfp, 0.5, None, ALU.mult).then_inc(s["rec_ready"], 1)
                dve.wait_ge(s["rowused"], NJ // GR)
                start, place = bank[4][:, 0:NT], bank[4][:, NT:2 * NT]
                token, column = view(12928, NT), view(13056, NT)
                link(dve.tensor_copy(token, start))
                dve.tensor_scalar(column, start, BIG, 1.0 / P, ALU.add, ALU.mult)
                link(dve.tensor_tensor(token, token, place, ALU.add))
                dve.tensor_scalar(sorti[:, :, 0], token, BIG, float(T - 1), ALU.add, ALU.min)
                dve.scalar_tensor_tensor(sorti[:, :, 1], place, float(NJ), column, ALU.mult, ALU.add)
                dve.tensor_scalar(sorti[:, :, 2], token, BIG, None, ALU.add).then_inc(s["sorted_sb"], 1)

            def ffn(ph):
                s = S[ph]
                dve.wait_ge(s["sorted_sb"], 1)
                if ph == 1:
                    for n in (1, 2, 4, 8, 16, 32):
                        double(n)
                dve.wait_ge(s["b2in"], 16)

                def expert(q):
                    return dve.value_load(eid[0:1, at(q, 1)], min_val=0, max_val=E - 1)

                def split_x(turn, k):
                    q, k, turn = tile(turn, k)
                    dve.wait_ge(s["turned"], q + 1)
                    if has(q, 2):
                        dve.wait_ge(s["m1"], q * 2 - 2)
                    src = bank[6 + k % 2][:, 0:DC * P].rearrange("p (c t) -> p c t", c=DC)
                    dve.tensor_scalar(xts[k % 2][:, 0], src, SX, None, ALU.mult).then_inc(s["xt_hi"], 1)
                    dve.wait_ge(s["xt_hi"], q + 1)
                    dve.scalar_tensor_tensor(xts[k % 2][:, 1], src, SX, xts[k % 2][:, 0], ALU.mult, ALU.subtract) \
                        .then_inc(s["xt"], 1)

                def split_h(turn, k):
                    q, k, turn = tile(turn, k)
                    e = expert(q)
                    if has(q, 2):
                        dve.wait_ge(s["m2"], q - 1)
                    for half in range(2):
                        f = slice(4 * half, 4 * half + 4)
                        dve.wait_ge(s["gelu"], q * 2 + half + 1)
                        sc = hscale[:, bass.ds(e, 1)]
                        dve.tensor_scalar(hs[k % 2][:, 0, f, :], hb[k % 2][:, f, :], sc, None, ALU.mult) \
                            .then_inc(s["h_hi"], 1)
                        dve.wait_ge(s["h_hi"], q * 2 + half + 1)
                        dve.scalar_tensor_tensor(hs[k % 2][:, 1, f, :], hb[k % 2][:, f, :], sc,
                                                 hs[k % 2][:, 0, f, :], ALU.mult, ALU.subtract).then_inc(s["hsplit"], 1)

                def result(turn, k):
                    _, before_k, before_turn = tile(turn, k - 2)
                    q, k, turn = tile(turn, k)
                    e = expert(q)
                    dve.wait_ge(s["m2"], q + 1)
                    if has(q, 2):
                        dve.wait_ge(s["scat"][before_k], before_turn * 16 + 16)
                    o, acc = og[k % 2], bank[4 + k % 2]
                    i2 = inv2[:, bass.ds(e, 1)]
                    dve.scalar_tensor_tensor(o, acc[:, D:2 * D], i2, b2b[:, bass.ds(e * D, D)], ALU.mult, ALU.add) \
                        .then_inc(s["o_chain"], 1)
                    dve.wait_ge(s["o_chain"], q * 2 + 1)
                    dve.scalar_tensor_tensor(o, acc[:, 0:D], i2, o, ALU.mult, ALU.add).then_inc(s["o_chain"], 1)
                    dve.wait_ge(s["o_chain"], q * 2 + 2)
                    dve.scalar_tensor_tensor(o, o, recf[:, k, 2:3], xg[k], ALU.mult, ALU.add).then_inc(s["o"], 1)

                def step(turn, k):
                    q = tile(turn, k)[0]
                    if not isinstance(q, int) or q + 2 < NT:
                        split_x(turn, k + 2)
                    if not isinstance(q, int) or q + 1 < NT:
                        split_h(turn, k + 1)
                    result(turn, k)

                split_x(0, 0)
                split_x(0, 1)
                split_h(0, 0)
                over_tiles(dve, step)

            route(1)
            ffn(1)

            for n in (64, 128, 256):
                double(n)
            link(dve.memset(state[:], 0.0))
            for c in range(-2, NC + LATE):
                if c >= LATE:
                    b = c - LATE
                    dve.wait_ge(s_lg, b + 1)
                    dve.tensor_copy(logits[:, b * CT:(b + 1) * CT, :],
                                    bank[5][:, 0:CT * E].rearrange("p (i e) -> p i e", e=E)).then_inc(s_lgsb, 1)
                if c == 0:
                    readout(0)
                    readout(1)
                if 0 <= c < NC:
                    dve.wait_ge(s_gs, c + 1)
                    dve.tensor_tensor(mod[:, 0, :], gs, turn[:, 0, :], ALU.mult).then_inc(s_in, 1)
                    dve.wait_ge(s_in, c + 1)
                    if c >= 1:
                        dve.wait_ge(s_aa, c)
                    dve.tensor_tensor_scan(zz[:, 0, :], rho[:].to_broadcast([P, CH]), mod[:, 0, :], state[:, 0:1],
                                           ALU.mult, ALU.add).then_inc(s_zr, 1)
                    dve.wait_ge(s_mi, c + 1)
                    dve.tensor_tensor_scan(zz[:, 1, :], rho[:].to_broadcast([P, CH]), mod[:, 1, :],
                                           state[:, 1:2], ALU.mult, ALU.add).then_inc(s_zi, 1)
                    dve.wait_ge(s_zr, c + 1)
                    dve.wait_ge(s_zi, c + 1)
                    zr, zi = zz[:, 0, CH - 1:CH], zz[:, 1, CH - 1:CH]
                    cl, sl = turn[:, 0, CH - 1:CH], turn[:, 1, CH - 1:CH]
                    dve.tensor_tensor(ev[:, 20:21], zi, sl, ALU.mult)
                    link(dve.tensor_tensor(ev[:, 21:22], zr, sl, ALU.mult))
                    dve.scalar_tensor_tensor(state[:, 0:1], zr, cl, ev[:, 20:21], ALU.mult, ALU.add)
                    dve.scalar_tensor_tensor(state[:, 1:2], zi, cl, ev[:, 21:22], ALU.mult, ALU.subtract)
                if c + 2 < NC:
                    n = c + 2
                    dve.wait_ge(sx[n % XS], 16 * (n // XS) + 16)
                    if n >= 2:
                        dve.wait_ge(s_nb, n - 1)
                    row_stats(xs[n % XS], n % 2, nm[:, n % 2, :], s_stats)
                if 1 <= c <= NC:
                    b = c - 1
                    dve.wait_ge(s_y, b + 1)
                    for h in range(2):
                        rows = xs[b % XS][:, 2 * h:2 * h + 2, :]
                        last = dve.tensor_tensor(rows, rows, bank[6 + h][:].rearrange("p (i d) -> p i d", d=D), ALU.add)
                    last.then_inc(s_x2, 1)
                    dve.wait_ge(s_x2, b + 1)
                    if b >= 2:
                        dve.wait_ge(s_nb3, b - 1)
                    row_stats(xs[b % XS], 2 + b % 2, nmean[:, b * CT:(b + 1) * CT], s_st3)
            dve.wait_ge(s_lgsb, NC)
            route(2)
            ffn(2)

        @block.tensor
        def _(pe):
            pe.wait_ge(const_done, 1)
            pe.wait_ge(par_in, 16 * NPAR)
            for c in range(DC):
                pe.transpose(bank[4][:, c * N:(c + 1) * N], braw[:, c * P:(c + 1) * P], ident[:])
                pe.transpose(bank[4][:, DC * N + c * P:DC * N + (c + 1) * P], craw[:, c, :], ident[:])
            pe.transpose(bank[5][:, 0:E * FC], b1raw, ident[0:E * FC, 0:E * FC]).then_inc(par_t, 1)

            def turn_rows(src, banks, done):
                for d in range(DC):
                    for i in range(CT):
                        last = pe.transpose(banks[d][:, i * P:(i + 1) * P], src[:, i, d * P:(d + 1) * P], ident[:])
                last.then_inc(done, 1)

            def route_logits(src, dst, done):
                for i in range(CT):
                    for d in range(DC):
                        last = pe.matmul(dst[:, i * E:(i + 1) * E], src[:, d, i * P:(i + 1) * P], wr[:, d, :],
                                         start=(d == 0), stop=(d == DC - 1))
                last.then_inc(done, 1)

            def entry(turn, k):
                c = chunk(turn, k)[0]
                pe.wait_ge(a_xn, c + 1)
                if has(c, 2):
                    pe.wait_ge(a_xt, c - 1)
                turn_rows(xnc[k], bank[2 * k:2 * k + 2], a_t)
                pe.wait_ge(a_xt, c + 1)
                if has(c, 2):
                    pe.wait_ge(a_lgsb, c - 1)
                route_logits(xtc, bank[6 + k][:, 0:CT * E], a_lg)
            Chain(pe, None).over_chunks(entry)

            def route(ph):
                s = S[ph]
                onehot = rt[3][:, 0:E * NJ // 2].bitcast(BF16)
                pe.wait_ge(s["onehot"], 1)
                pe.matmul(bank[5][:, 0:256], earlier[:], onehot, start=True, stop=True)
                pe.matmul(bank[5][:, 256:512], ones[:], onehot, start=True, stop=True).then_inc(s["counts"], 1)
                pe.wait_ge(s["pos"], 1)
                pe.wait_ge(s["starts"], 1)
                for g in range(NJ // GR):
                    pe.wait_ge(s["row"], g + 1)
                    for i in range(GR):
                        j = GR * g + i
                        last = pe.matmul(bank[4][:, 0:2 * NT], onerow[:, j, :], sval[:, j, :, :].rearrange("p a b -> p (a b)"),
                                         start=(j == 0), stop=(j == NJ - 1))
                    last.then_inc(s["rowused"], 1)
                pe.wait_ge(s["sorted_sb"], 1)

            def ffn(ph):
                s = S[ph]

                def turn_tile(turn, k):
                    q, k, turn = tile(turn, k)
                    pe.wait_ge(s["xn"], q + 1)
                    if has(q, 2):
                        pe.wait_ge(s["xt"], q - 1)
                    for d in range(DC):
                        last = pe.transpose(bank[6 + k % 2][:, d * P:(d + 1) * P], xng[k % 2][:, d * P:(d + 1) * P],
                                            ident[:])
                    last.then_inc(s["turned"], 1)

                def expert(q):
                    e = pe.value_load(eid[0:1, at(q, 1)], min_val=0, max_val=E - 1)
                    return pe.snap(e * (2 * WB))

                def product1(turn, k, w):
                    q, k, turn = tile(turn, k)
                    pe.wait_ge(s["xt"], q + 1)
                    for half in range(2):
                        acc = bank[2 * (k % 2) + half]
                        if has(q, 2):
                            pe.wait_ge(s["gelu"], q * 2 - 3 + half)
                        for f in range(4 * half, 4 * half + 4):
                            weights = [big[:, bass.ds(w + 2 * (wpart * WE + d * F + f * P), 2 * P)].bitcast(F16)
                                       for wpart in range(2) for d in range(DC)]
                            for block_of in weights:
                                pe.lower_ap(block_of, for_matmul_weights=True)
                            n = 0
                            for wpart in range(2):
                                for d in range(DC):
                                    for xpart in range(2 - wpart):
                                        last = pe.matmul(acc[:, (f % 4) * P:(f % 4 + 1) * P], weights[wpart * DC + d],
                                                         xts[k % 2][:, xpart, d, :], start=(n == 0), stop=(n == 5))
                                        n += 1
                        last.then_inc(s["m1"], 1)

                def product2(turn, k, w):
                    q, k, turn = tile(turn, k)
                    acc = bank[4 + k % 2]
                    if has(q, 2):
                        pe.wait_ge(s["o"], q - 1)
                    for f in range(FC):
                        if f % 4 == 0:
                            pe.wait_ge(s["hsplit"], q * 2 + f // 4 + 1)
                            both = [big[:, bass.ds(w + (WB + g * 4 * D), 4 * D)].bitcast(F16) for g in range(f, f + 4)]
                            for block_of in both:
                                pe.lower_ap(block_of)
                        rhs = both[f % 4]
                        pe.matmul(acc[:], hs[k % 2][:, 0, f, :], rhs, start=(f == 0), stop=False)
                        last = pe.matmul(acc[:, 0:D], hs[k % 2][:, 1, f, :], rhs[:, 0:D], start=False, stop=(f == FC - 1))
                    last.then_inc(s["m2"], 1)

                def step(turn, k):
                    q = tile(turn, k)[0]
                    w = expert(q)
                    if not isinstance(q, int) or q + 1 < NT:
                        w_next = expert(q + 1)
                    if not isinstance(q, int) or q + 2 < NT:
                        turn_tile(turn, k + 2)
                    if not isinstance(q, int) or q + 1 < NT:
                        product1(turn, k + 1, w_next)
                    product2(turn, k, w)

                turn_tile(0, 0)
                turn_tile(0, 1)
                product1(0, 0, expert(0))
                over_tiles(pe, step)

            route(1)
            ffn(1)
            for c in range(-1, NC + 3):
                if 1 <= c <= NC:
                    b = c - 1
                    pe.wait_ge(s_hr, b + 1)
                    if b >= 1:
                        pe.wait_ge(s_x2, b)
                    for i in range(CT):
                        last = pe.matmul(bank[6 + i // 2][:, (i % 2) * D:(i % 2 + 1) * D],
                                         hr[b % 2][:, i * P:(i + 1) * P], ct[:], start=True, stop=True)
                    last.then_inc(s_y, 1)
                if c + 1 < NC:
                    n = c + 1
                    pe.wait_ge(s_un, n + 1)
                    if n >= 1:
                        pe.wait_ge(s_uts, n)
                    turn_rows(uns[n % 2], bank[0:2], s_ut)
                if c >= 3:
                    b = c - 3
                    pe.wait_ge(s_xt3, b + 1)
                    if b >= 1:
                        pe.wait_ge(s_lgsb, b)
                    route_logits(xt3, bank[5][:, 0:CT * E], s_lg)
                if c + 1 < NC:
                    pe.wait_ge(s_uts, n + 1)
                    if n >= 1:
                        pe.wait_ge(s_gs, n)
                    for d in range(DC):
                        last = pe.matmul(bank[4][:], bt[:, d, :], uts[:, d, :], start=(d == 0), stop=(d == DC - 1))
                    last.then_inc(s_g, 1)
                if 2 <= c < NC + 2:
                    b = c - 2
                    pe.wait_ge(s_xn3, b + 1)
                    if b >= 1:
                        pe.wait_ge(s_xt3, b)
                    turn_rows(xn3[b % 2], bank[2:4], s_t3)
            route(2)
            ffn(2)


INPUTS = ("L0_attn_u L0_attn_A_real L0_attn_A_imag L0_attn_B L0_attn_C L0_ffn_Wr L0_ffn_W1 L0_ffn_b1 L0_ffn_W2 "
          "L0_ffn_b2").split()


def kernel(**inputs):
    import concourse.bacc as bacc
    import numpy as np
    from concourse.bass_utils import run_bass_kernel_spmd

    nc = bacc.Bacc("TRN2", target_bir_lowering=False, num_devices=1)
    arrays = {name: np.ascontiguousarray(inputs[name]) for name in INPUTS}
    aps = {name: nc.dram_tensor(name, a.shape, F32, kind="ExternalInput").ap() for name, a in arrays.items()}
    aps["out"] = nc.dram_tensor("out", (1, T, D), F32, kind="ExternalOutput").ap()
    macaron(nc, aps)
    return run_bass_kernel_spmd(nc, [arrays], core_ids=[0]).results[0]["out"]
```
